# Optimizing a Trainium2 kernel written in Bass

```python
import numpy as np
import jax
import jax.numpy as jnp

def _softmax(x, axis=-1):
    return jax.nn.softmax(x, axis=axis)
def _gelu(x):
    return jax.nn.gelu(x, approximate=True)
def _silu(x):
    return jax.nn.silu(x)
def _sigmoid(x):
    return jax.nn.sigmoid(x)
def _layernorm(x, axis=-1, eps=1e-5):
    m = jnp.mean(x, axis=axis, keepdims=True)
    v = jnp.var(x, axis=axis, keepdims=True)
    return (x - m) / jnp.sqrt(v + eps)
def _scatter_add(tgt, idx, src, axis=0):
    return tgt.at[idx].add(src)
def _segment_sum(src, seg, n):
    return jax.ops.segment_sum(src, seg, n)

kernel_name = 'mk_conv_preact_d2_conv_nchw256_49dd4a'

def setup_inputs(seed: int = 0):
    np.random.seed(seed)
    _w = jnp.asarray
    def _rec_inputs():
        import jax
        import jax.numpy as jnp
        _gk = jax.random.key(seed)
        x = -0.0002023 + 1 * jax.random.normal(jax.random.fold_in(_gk, 1), (8, 256, 56, 56), jnp.float32)
        return x
    x = _rec_inputs()
    def _L0_conv_setup():
        import jax, jax.numpy as jnp
        import numpy as np
        KH, KW = (3, 3)
        PAD = 1
        STRIDE = 1
        IN_CH, OUT_CH = (256, 256)
        SPARSITY = 0.9
        key = jax.random.key(seed)
        kx, kw, km = jax.random.split(key, 3)
        x = jax.random.normal(kx, (8, IN_CH, 56, 56), dtype=jnp.float32)
        in_feats = IN_CH * KH * KW
        w_dense = jax.random.normal(kw, (OUT_CH, in_feats), dtype=jnp.float32) * 0.05
        mask = (jax.random.uniform(km, (OUT_CH, in_feats)) > SPARSITY).astype(jnp.float32)
        weight = w_dense * mask
        return {'x': x, 'weight': weight}
    _L0_conv_all = _L0_conv_setup()
    _L0_conv_in = {k: v for k, v in _L0_conv_all.items() if k in ('weight', )}
    del _L0_conv_all

    def _L1_conv_setup():
        import jax, jax.numpy as jnp
        from jax import lax
        import numpy as np
        WS = 4
        DIM = 8
        HEADS = 32
        TOT = 256
        CIN = 256
        COUT = 256
        NS = 1
        BN_EPS = 1e-05

        def _avg_pool5(x):
            s = lax.reduce_window(x, 0.0, lax.add, (1, 1, 5, 5), (1, 1, 1, 1), [(0, 0), (0, 0), (2, 2), (2, 2)])
            return s / 25.0
        key = jax.random.key(seed)
        k0, k1, k2 = jax.random.split(key, 3)
        B, H, W = (4, 192, 192)
        x = jax.random.normal(k0, (B, CIN, H, W), jnp.float32)
        qkv_w = jax.random.normal(k1, (3 * TOT, CIN), jnp.float32) * 0.02
        proj_w = jax.random.normal(k2, (COUT, TOT * (1 + NS)), jnp.float32) * 0.02
        bn_gamma = jnp.ones((COUT,), jnp.float32)
        bn_beta = jnp.zeros((COUT,), jnp.float32)
        bn_mean = jnp.zeros((COUT,), jnp.float32)
        bn_var = jnp.ones((COUT,), jnp.float32)
        return {'x': x, 'qkv_w': qkv_w, 'proj_w': proj_w, 'bn_gamma': bn_gamma, 'bn_beta': bn_beta, 'bn_mean': bn_mean, 'bn_var': bn_var}
    _L1_conv_all = _L1_conv_setup()
    _L1_conv_in = {k: v for k, v in _L1_conv_all.items() if k in ('qkv_w', 'proj_w', 'bn_gamma', 'bn_beta', 'bn_mean', 'bn_var', )}
    del _L1_conv_all

    return {
        "x": x,
        "L0_conv_weight": _L0_conv_in["weight"],
        "L1_conv_qkv_w": _L1_conv_in["qkv_w"],
        "L1_conv_proj_w": _L1_conv_in["proj_w"],
        "L1_conv_bn_gamma": _L1_conv_in["bn_gamma"],
        "L1_conv_bn_beta": _L1_conv_in["bn_beta"],
        "L1_conv_bn_mean": _L1_conv_in["bn_mean"],
        "L1_conv_bn_var": _L1_conv_in["bn_var"],
    }

def reference(x, L0_conv_weight, L1_conv_qkv_w, L1_conv_proj_w, L1_conv_bn_gamma, L1_conv_bn_beta, L1_conv_bn_mean, L1_conv_bn_var):
    import jax
    import jax.numpy as jnp
    def _L0_conv_ref(x, weight):
        import jax, jax.numpy as jnp
        import numpy as np
        KH, KW = (3, 3)
        PAD = 1
        STRIDE = 1
        IN_CH, OUT_CH = (256, 256)
        SPARSITY = 0.9
        patches = jax.lax.conv_general_dilated_patches(x, filter_shape=(KH, KW), window_strides=(STRIDE, STRIDE), padding=((PAD, PAD), (PAD, PAD)))
        B, F, Ho, Wo = patches.shape
        out = jnp.einsum('of,bfp->bop', weight, patches.reshape(B, F, Ho * Wo))
        return out.reshape(B, weight.shape[0], Ho, Wo)

    def _L1_conv_ref(x, qkv_w, proj_w, bn_gamma, bn_beta, bn_mean, bn_var):
        import jax, jax.numpy as jnp
        from jax import lax
        import numpy as np
        WS = 4
        DIM = 8
        HEADS = 32
        TOT = 256
        CIN = 256
        COUT = 256
        NS = 1
        BN_EPS = 1e-05

        def _avg_pool5(x):
            s = lax.reduce_window(x, 0.0, lax.add, (1, 1, 5, 5), (1, 1, 1, 1), [(0, 0), (0, 0), (2, 2), (2, 2)])
            return s / 25.0
        B, C, H, W = x.shape
        ws = WS
        Hn, Wn = (H // ws, W // ws)
        xw = x.reshape(B, C, Hn, ws, Wn, ws).transpose(0, 2, 4, 1, 3, 5)
        xw = xw.reshape(-1, C, ws, ws)
        N = xw.shape[0]
        qkv = jnp.einsum('nchw,oc->nohw', xw, qkv_w)
        pooled = _avg_pool5(qkv)
        msq = jnp.concatenate([qkv, pooled], axis=1)
        msq = msq.reshape(N, -1, 3 * DIM, ws * ws).transpose(0, 1, 3, 2)
        q = jax.nn.relu(msq[..., :DIM])
        k = jax.nn.relu(msq[..., DIM:2 * DIM])
        v = msq[..., 2 * DIM:]
        v = jnp.pad(v, ((0, 0), (0, 0), (0, 0), (0, 1)), constant_values=1.0)
        kv = jnp.einsum('ngld,nglm->ngdm', k, v)
        out = jnp.einsum('ngld,ngdm->nglm', q, kv)
        out = out[..., :-1] / (out[..., -1:] + 1e-15)
        out = out.transpose(0, 1, 3, 2).reshape(N, -1, ws, ws)
        Cw = out.shape[1]
        out = out.reshape(B, Hn, Wn, Cw, ws, ws).transpose(0, 3, 1, 4, 2, 5)
        out = out.reshape(B, Cw, H, W)
        y = jnp.einsum('nchw,oc->nohw', out, proj_w)
        inv = bn_gamma / jnp.sqrt(bn_var + BN_EPS)
        y = y * inv[None, :, None, None] + (bn_beta - bn_mean * inv)[None, :, None, None]
        return y

    def _gn(v, G=32, eps=1e-5):
        B_, C_, H_, W_ = v.shape
        g = v.reshape(B_, G, C_ // G, H_, W_)
        m = jnp.mean(g, axis=(2, 3, 4), keepdims=True)
        s = jnp.var(g, axis=(2, 3, 4), keepdims=True)
        return ((g - m) / jnp.sqrt(s + eps)).reshape(v.shape)

    def _ln_c(v, eps=1e-6):
        m = jnp.mean(v, axis=1, keepdims=True)
        s = jnp.var(v, axis=1, keepdims=True)
        return (v - m) / jnp.sqrt(s + eps)

    def _ln_t(v, eps=1e-5):
        m = jnp.mean(v, axis=-1, keepdims=True)
        s = jnp.var(v, axis=-1, keepdims=True)
        return (v - m) / jnp.sqrt(s + eps)

    def _to_tokens(v):
        B_, C_, H_, W_ = v.shape
        return v.reshape(B_, C_, H_ * W_).transpose(0, 2, 1)
    def _from_tokens(t, like):
        B_, C_, H_, W_ = like.shape
        return t.transpose(0, 2, 1).reshape(B_, C_, H_, W_)

    x = x + _L0_conv_ref(_gn(x), L0_conv_weight)
    x = x + _L1_conv_ref(_gn(x), L1_conv_qkv_w, L1_conv_proj_w, L1_conv_bn_gamma, L1_conv_bn_beta, L1_conv_bn_mean, L1_conv_bn_var)
    return x


_drawn_inputs = setup_inputs


def setup_inputs(seed=0):
    import zlib

    import numpy as np

    out = dict(_drawn_inputs(seed))
    spreads = {'L1_conv_bn_gamma': (1.0, 0.6),
     'L1_conv_bn_beta': (0.0, 0.1),
     'L1_conv_bn_mean': (0.0, 0.1),
     'L1_conv_bn_var': (1.0, 0.6)}
    factors = {}
    for name, (base, spread) in spreads.items():
        noise = np.random.default_rng([zlib.crc32(name.encode()), seed]).standard_normal(out[name].shape)
        drawn = base * np.exp(spread * noise) if base else spread * noise
        out[name] = jnp.asarray(drawn.astype(out[name].dtype))
    for name, factor in factors.items():
        out[name] = (out[name] * factor).astype(out[name].dtype)
    return out
```

```python
import numpy as np

import concourse.bass as bass
from concourse import mybir
from contextlib import ExitStack

F32 = mybir.dt.float32
ALU = mybir.AluOpType
ACT = mybir.ActivationFunctionType

B, C, H, W = 8, 256, 56, 56
P = 128
KT = C // P
MT = C // P
HW = H * W
TAPS = 9
PADW = W + 2
WS = 4
TOK = WS * WS
WIN_PER_ROW = W // WS
ROWS = H // WS
ROW_TOK = WIN_PER_ROW * TOK
NWIN = WIN_PER_ROW // 2
TT = NWIN * TOK
TILES = 2 * ROWS
CHUNK_H = 2 * WS
CHUNKS = H // CHUNK_H
CHUNK = CHUNK_H * W
DIM = 8
G = 2 * C // P
HEADS_G = P // DIM
QUADS = P // 32
HEADS_Q = 32 // DIM
KVW = QUADS * HEADS_Q * (DIM + 1)
QW = HEADS_Q * (DIM + 1)
SLOTS = NWIN + 1
GN_GROUP = C // 32
GN_EPS = 1e-5
BN_EPS = 1e-5
DEN_EPS = 1e-15
POOL_SCALE = 1.0 / 25.0
BATCHES = ((0, 3), (3, 2), (5, 2))
T_A = 4
DMA = 16

CONSTS = 9

BANK_Q = 0
BANK_TA = 1
BANK_KV = 2
BANK_S = (3, 4)
BANK_O = (5, 6, 7)
BANK_TB = 7
BANK_C = (5, 6)

PLACE = {"act": ((0, 0), (0, 1), (1, 0)), "pool": ((0, 2), (0, 3)), "dve": ((1, 1), (1, 2), (1, 3))}


def build(nc, x, w_conv, w_q, w_kv, w_proj, bn, gavg, pool_m, ident, hmask, vinit, out):
    ctx = ExitStack()
    with ctx:
        def sb(name, shape):
            return ctx.enter_context(nc.sbuf_tensor(name, shape, F32))

        def sem(name):
            return ctx.enter_context(nc.semaphore(name))

        wc = sb("wc", [P, KT, TAPS, C])
        wq = sb("wq", [P, KT, C])
        wkv = sb("wkv", [P, KT, 2 * C])
        wp = sb("wp", [P, G, C])
        bnp = sb("bnp", [P, 4, MT])
        gav = sb("gav", [P, P])
        poolm = sb("poolm", [TT, TT])
        idn = sb("idn", [P, P])
        hm = sb("hm", [P, HEADS_Q])
        xs = sb("xs", [P, 2, KT, HW])
        xp = sb("xp", [P, KT, H + 2, PADW])
        st0 = sb("st0", [P, KT, CHUNKS, 6])
        st1 = sb("st1", [P, KT, CHUNKS, 6])
        mv = sb("mv", [P, KT, 2])
        dev = sb("dev", [P, 8, KT])
        gn0 = sb("gn0", [P, 2, KT])
        gn1 = sb("gn1", [P, 2, KT])
        bni = sb("bni", [P, MT])
        bns = sb("bns", [P, MT])
        bnt = sb("bnt", [P, 6, MT])
        xh = sb("xh", [P, 2, KT, ROW_TOK])
        qs = sb("qs", [P, G, 2, ROW_TOK + TOK])
        qraw = sb("qraw", [P, MT * ROW_TOK])
        qh = sb("qh", [P, MT * ROW_TOK])
        qm = sb("qm", [P, MT * ROW_TOK // 4])
        qsum = sb("qsum", [P, MT * ROW_TOK])
        raw = sb("raw", [TT, 2, 3 * C])
        kr = sb("kr", [TT, 2, 2 * C])
        ve = sb("ve", [TT, SLOTS, 2, C])
        kvm = sb("kvm", [P, 2, 2, SLOTS, QW])
        kvb = sb("kvb", [P, G, NWIN, KVW])
        den = sb("den", [P, NWIN, HEADS_G])
        rcp = sb("rcp", [P, NWIN, HEADS_G])
        ao = sb("ao", [P, NWIN, P])
        at = sb("at", [P, G, 2, ROW_TOK])
        yb = sb("yb", [P, MT, ROW_TOK])

        ps = ctx.enter_context(nc.psum_tensor("ps", [P, 8, 512], F32))

        x_loaded = sem("x_loaded")
        w_loaded = sem("w_loaded")
        c_loaded = sem("c_loaded")
        ve_loaded = sem("ve_loaded")
        stored = sem("stored")
        conv_done = sem("conv_done")
        gsum_done = sem("gsum_done")
        kv_done = sem("kv_done")
        pool_done = sem("pool_done")
        q_done = sem("q_done")
        ktv_done = sem("ktv_done")
        att_done = sem("att_done")
        tr_done = sem("tr_done")
        proj_done = sem("proj_done")
        raw_ready = sem("raw_ready")
        kp_ready = sem("kp_ready")
        vp_ready = sem("vp_ready")
        placed = {e: sem("placed_" + e) for e in PLACE}
        q_ready = sem("q_ready")
        qraw_ready = sem("qraw_ready")
        at_ready = sem("at_ready")
        y_ready = sem("y_ready")
        root_ready = sem("root_ready")
        set_up = sem("set_up")
        conv_added = sem("conv_added")
        gn_in = sem("gn_in")
        gn_step = sem("gn_step")
        gn_var = sem("gn_var")
        xp_ready = sem("xp_ready")
        st0_done = sem("st0_done")
        st1_done = sem("st1_done")
        bn_ready = sem("bn_ready")
        bn_step = sem("bn_step")
        xh_ready = sem("xh_ready")
        k_ready = sem("k_ready")
        masked = sem("masked")
        den_ready = sem("den_ready")
        rcp_ready = sem("rcp_ready")
        ao_ready = sem("ao_ready")
        qp_ready = sem("qp_ready")
        pad_ready = sem("pad_ready")
        q_step = sem("q_step")
        qsum_ready = sem("qsum_ready")
        out_ready = sem("out_ready")

        block = ctx.enter_context(nc.Block())

        N_ACT, N_POOL, N_DVE = (len(PLACE[e]) for e in ("act", "pool", "dve"))

        def slots(eng, b, slot, last):
            slot(b * TILES - 1, b * ROWS, -1, b, 0, last)
            for t in range(4):
                slot(b * TILES + t, b * ROWS, t, b, 0, last)
            with eng.Fori(1, CHUNKS - 1) as c:
                for t in range(4):
                    slot(b * TILES + c * 4 + t, b * ROWS + c * 2, 4 + t, b, c, last)
            for i in range(TILES - 4, TILES + 3):
                slot(b * TILES + i, b * ROWS + (i // 4) * 2, i, b, i // 4, last)

        def grow(R0, i, r):
            return R0 + (r - (2 * (i // 4) if i >= 0 else 0))

        def lrow(c, i, r):
            return c * 2 + (r - (2 * (i // 4) if i >= 0 else 0))

        def xs_row(par, mt, row, n=ROW_TOK):
            return xs[:, bass.ds(par, 1), mt, bass.ds(row * ROW_TOK, n)]

        def alone(eng, value):
            value = value if isinstance(value, int) else eng.to_reg(value)
            eng.wait_ge(c_loaded, DMA)
            return value

        @block.sync
        def _(sp):
            def load_x(img):
                for kt in range(KT):
                    sp.dma_start(xs[:, bass.ds(img % 2, 1), kt, :],
                                 x[bass.ds(img, 1), kt * P:(kt + 1) * P, :].rearrange("o p n -> p o n")).then_inc(x_loaded, DMA)

            load_x(0)
            for dst, src in ((gav, gavg), (bnp, bn)):
                sp.dma_start(dst[:], src).then_inc(c_loaded, DMA)
            for kt in range(KT):
                sp.dma_start(wc[:, kt], w_conv[:, kt]).then_inc(w_loaded, DMA)
            for dst, src in ((wq, w_q), (wkv, w_kv), (wp, w_proj), (poolm, pool_m), (idn, ident), (hm, hmask)):
                sp.dma_start(dst[:], src).then_inc(c_loaded, DMA)
            sp.dma_start(ve[:], vinit).then_inc(c_loaded, DMA)
            sp.wait_ge(c_loaded, CONSTS * DMA)
            sp.wait_ge(x_loaded, KT * DMA)
            load_x(1)

            def slot(T, R0, i, b, c, last):
                if i + 1 < TILES:
                    par = (i + 1) % 2
                    sp.wait_ge(vp_ready, alone(sp, T + 2))
                    if i >= 0:
                        sp.wait_ge(ktv_done, alone(sp, 2 * T + 2))
                    for w in range(NWIN):
                        sp.dma_start(ve[w * TOK:(w + 1) * TOK, w].rearrange("p h c -> p (h c)"),
                                     raw[w * TOK:(w + 1) * TOK, par, C:3 * C]).then_inc(ve_loaded, DMA)
                if i % 2 == 0 and 0 <= (i - 4) // 2 < ROWS:
                    r = (i - 4) // 2
                    sp.wait_ge(out_ready, alone(sp, grow(R0, i, r) + 1))
                    row = lrow(c, i, r)
                    for mt in range(MT):
                        sp.dma_start(out[bass.ds(b, 1), mt * P:(mt + 1) * P, bass.ds(row * ROW_TOK, ROW_TOK)]
                                     .rearrange("o p n -> p o n"),
                                     xs_row(b % 2, mt, row)).then_inc(stored, DMA)

            with sp.Fori(0, B - 2) as b:
                slots(sp, b, slot, False)
                sp.wait_ge(stored, alone(sp, (b + 1) * (MT * ROWS * DMA)))
                load_x(b + 2)
            with sp.Fori(B - 2, B) as b:
                slots(sp, b, slot, False)
            sp.wait_ge(stored, B * MT * ROWS * DMA)

        @block.tensor
        def _(pe):
            def conv(img):
                pe.wait_ge(xp_ready, alone(pe, img + 1))
                with pe.Fori(0, CHUNKS) as c:
                    for mt in range(MT):
                        n = (img * CHUNKS + c) * MT + mt
                        pe.wait_ge(conv_added, n + 1)
                        k = 0
                        for kt in range(KT):
                            for tap in range(TAPS):
                                dy, dx = tap // 3, tap % 3
                                last = nc.tensor.matmul(
                                    ps[:, BANK_C[mt], 0:CHUNK], wc[:, kt, tap, mt * P:(mt + 1) * P],
                                    xp[:, kt, bass.ds(c * CHUNK_H + dy, CHUNK_H), dx:dx + W],
                                    start=(k == 0), stop=(k == KT * TAPS - 1))
                                k += 1
                        last.then_inc(conv_done, 1)

            def group_sums(n):
                for s in range(2):
                    pe.wait_ge(gn_in, 2 * n + s + 1)
                    src = mv[:, :, 0] if s == 0 else dev[:, 1, :]
                    nc.tensor.matmul(ps[:, BANK_Q, s * KT:(s + 1) * KT], gav[:], src,
                                     start=True, stop=True).then_inc(gsum_done, 1)

            def slot(T, R0, i, b, c, last_image):
                par1, par = (i + 1) % 2, i % 2
                if i + 1 < TILES:
                    rp = ((i + 1) // 2) % 2
                    if i % 2 == 1:
                        pe.wait_ge(xh_ready, grow(R0, i, (i + 1) // 2) + 1)
                    if i >= 0:
                        pe.wait_ge(vp_ready, T + 1)
                    off = ((i + 1) % 2) * TT
                    for kt in range(KT):
                        last = nc.tensor.matmul(ps[0:TT, BANK_KV, :], xh[:, rp, kt, off:off + TT],
                                                wkv[:, kt, :], start=(kt == 0), stop=(kt == KT - 1))
                    last.then_inc(kv_done, 1)
                if 1 <= i <= TILES:
                    j = i - 1
                    rp, off = (j // 2) % 2, (j % 2) * TT
                    pe.wait_ge(placed["act"], N_ACT * T)
                    pe.wait_ge(placed["pool"], N_POOL * T)
                    pe.wait_ge(placed["dve"], N_DVE * T)
                    pe.wait_ge(q_ready, grow(R0, i, j // 2) + 1)
                    pe.wait_ge(qp_ready, grow(R0, i, j // 2) + 1)
                    for n, (w0, nw) in enumerate(BATCHES):
                        if j >= 1:
                            pe.wait_ge(ao_ready, 3 * T + (n - 5))
                            if BANK_O[n] == BANK_TB:
                                pe.wait_ge(at_ready, 2 * T - 2)
                        for w in range(w0, w0 + nw):
                            for g in range(G):
                                o = off + w * TOK
                                last = nc.tensor.matmul(
                                    ps[32 * g:32 * g + 32, BANK_O[n], (w - w0) * KVW:(w - w0 + 1) * KVW],
                                    qs[:, g, rp, o:o + 2 * TOK], kvb[:, g, w, :], start=True, stop=True)
                        last.then_inc(att_done, 1)
                if i + 1 < TILES:
                    pe.wait_ge(raw_ready, T + 2)
                    nc.tensor.matmul(ps[0:TT, BANK_KV, :], poolm[:], raw[:, par1, 0:2 * C],
                                     start=True, stop=True).then_inc(pool_done, 1)
                if 0 <= i < TILES:
                    for h in range(2):
                        pe.wait_ge(ve_loaded, (T + 1) * (NWIN * DMA))
                        pe.wait_ge(k_ready if h == 0 else kp_ready, T + 1)
                        if i >= 1:
                            pe.wait_ge(masked, 2 * T + (h - 1))
                        for gg in range(2):
                            for q in range(QUADS):
                                k0 = h * C + gg * P + 32 * q
                                v0 = gg * P + 32 * q
                                last = nc.tensor.matmul(
                                    ps[32 * q:32 * q + 32, BANK_S[h], gg * C:(gg + 1) * C],
                                    kr[:, par, k0:k0 + 32], ve[:, :, h, v0:v0 + 32], start=True, stop=True)
                        last.then_inc(ktv_done, 1)
                if i % 2 == 1 and i + 1 < TILES:
                    r = (i + 1) // 2
                    if i >= 5:
                        pe.wait_ge(y_ready, grow(R0, i, (i - 5) // 2) + 1)
                    for mt in range(MT):
                        for kt in range(KT):
                            last = nc.tensor.matmul(ps[:, BANK_Q, mt * ROW_TOK:(mt + 1) * ROW_TOK],
                                                    wq[:, kt, mt * P:(mt + 1) * P], xh[:, r % 2, kt, :],
                                                    start=(kt == 0), stop=(kt == KT - 1))
                    last.then_inc(q_done, 1)
                if 1 <= i <= TILES:
                    for n, (w0, w1) in enumerate(((0, T_A), (T_A, NWIN))):
                        pe.wait_ge(ao_ready, 3 * T + (n - 1))
                        if n == 0 and i >= 2:
                            pe.wait_ge(at_ready, 2 * T - 3)
                        for w in range(w0, w1):
                            last = nc.tensor.transpose(ps[:, BANK_TA if n == 0 else BANK_TB, (w - w0) * P:(w - w0 + 1) * P],
                                                       ao[:, w, :], idn[:])
                        last.then_inc(tr_done, 1)
                if i % 2 == 0 and 0 <= (i - 4) // 2 < ROWS:
                    r = (i - 4) // 2
                    pe.wait_ge(at_ready, 2 * T - 4)
                    if i == TILES and not last_image:
                        pe.wait_ge(gn_var, 2 * b + 3)
                    if i < TILES:
                        pe.wait_ge(q_ready, grow(R0, i, i // 2) + 1)
                        pe.wait_ge(qraw_ready, grow(R0, i, i // 2) + 1)
                    else:
                        pe.wait_ge(y_ready, grow(R0, i, r))
                    for mt in range(MT):
                        for g in range(G):
                            last = nc.tensor.matmul(ps[:, BANK_Q, mt * ROW_TOK:(mt + 1) * ROW_TOK],
                                                    wp[:, g, mt * P:(mt + 1) * P], at[:, g, r % 2, :],
                                                    start=(g == 0), stop=(g == G - 1))
                    last.then_inc(proj_done, 1)
                if i == TILES - 1 and not last_image:
                    pe.wait_ge(y_ready, grow(R0, i, (i - 5) // 2) + 1)
                    group_sums(2 * b + 2)

            pe.wait_ge(c_loaded, CONSTS * DMA)
            group_sums(0)
            pe.wait_ge(w_loaded, KT * DMA)
            conv(0)
            group_sums(1)
            with pe.Fori(0, B - 1) as b:
                slots(pe, b, slot, False)
                conv(b + 1)
                pe.wait_ge(y_ready, (b + 1) * ROWS)
                pe.wait_ge(at_ready, (b + 1) * (2 * TILES))
                group_sums(2 * b + 3)
            slots(pe, B - 1, slot, True)

        @block.scalar
        def _(act):
            def root(n):
                act.wait_ge(gn_var, n + 1)
                nc.scalar.activation(dev[:, 3, :], dev[:, 2, :], ACT.Sqrt).then_inc(root_ready, 1)

            def slot(T, R0, i, b, c, last_image):
                par1 = (i + 1) % 2
                if i + 1 < TILES:
                    act.wait_ge(kv_done, T + 2)
                    if i >= 1:
                        act.wait_ge(pool_done, T)
                        act.wait_ge(k_ready, T)
                        act.wait_ge(ve_loaded, T * (NWIN * DMA))
                    nc.scalar.copy(raw[:, par1, 0:2 * C], ps[0:TT, BANK_KV, :]).then_inc(raw_ready, 1)
                    act.wait_ge(pool_done, T + 2)
                    if i >= 1:
                        act.wait_ge(ktv_done, 2 * T)
                    nc.scalar.activation(kr[:, par1, C:2 * C], ps[0:TT, BANK_KV, 0:C], ACT.Relu,
                                         scale=POOL_SCALE).then_inc(kp_ready, 1)
                    nc.scalar.activation(raw[:, par1, 2 * C:3 * C], ps[0:TT, BANK_KV, C:2 * C], ACT.Copy,
                                         scale=POOL_SCALE).then_inc(vp_ready, 1)
                if 0 <= i < TILES:
                    for h, q in PLACE["act"]:
                        act.wait_ge(masked, 2 * T + (h + 1))
                        if i >= 1:
                            act.wait_ge(att_done, 3 * T)
                        s = slice(32 * q, 32 * q + 32)
                        nc.scalar.copy(kvb[s, 2 * h:2 * h + 2, :, q * QW:(q + 1) * QW],
                                       kvm[s, h, :, 0:NWIN, :]).then_inc(placed["act"], 1)
                if i % 2 == 1 and i + 1 < TILES:
                    r = (i + 1) // 2
                    act.wait_ge(q_done, grow(R0, i, r) + 1)
                    if i >= 3:
                        act.wait_ge(att_done, 3 * T - 3)
                    nc.scalar.activation(qs[:, 0:MT, r % 2, 0:ROW_TOK],
                                         ps[:, BANK_Q, 0:MT * ROW_TOK].rearrange("p (m n) -> p m n", m=MT),
                                         ACT.Relu).then_inc(q_ready, 1)
                    if i >= 1:
                        act.wait_ge(qsum_ready, grow(R0, i, r))
                    nc.scalar.copy(qraw[:], ps[:, BANK_Q, 0:MT * ROW_TOK]).then_inc(qraw_ready, 1)
                if 1 <= i <= TILES:
                    j = i - 1
                    rp, off = (j // 2) % 2, (j % 2) * TT
                    for n, (w0, w1) in enumerate(((0, T_A), (T_A, NWIN))):
                        act.wait_ge(tr_done, 2 * T + (n - 1))
                        src = ps[:, BANK_TA if n == 0 else BANK_TB, 0:(w1 - w0) * P]
                        nc.scalar.copy(
                            at[:, :, rp, off + w0 * TOK:off + w1 * TOK].rearrange("p g (w t) -> p w g t", t=TOK),
                            src.rearrange("p (w g t) -> p w g t", g=G, t=2 * TOK)[:, :, :, 0:TOK]).then_inc(at_ready, 1)
                if i % 2 == 0 and 0 <= (i - 4) // 2 < ROWS:
                    r = (i - 4) // 2
                    act.wait_ge(proj_done, grow(R0, i, r) + 1)
                    if r >= 1:
                        act.wait_ge(out_ready, grow(R0, i, r))
                    for mt in range(MT):
                        last = nc.scalar.activation(yb[:, mt, :], ps[:, BANK_Q, mt * ROW_TOK:(mt + 1) * ROW_TOK],
                                                    ACT.Identity, bias=bns[:, mt:mt + 1], scale=bni[:, mt:mt + 1])
                    last.then_inc(y_ready, 1)
                if i == TILES and not last_image:
                    root(2 * b + 2)

            act.wait_ge(bn_step, 1)
            nc.scalar.activation(bnt[:, 1, :], bnt[:, 0, :], ACT.Sqrt).then_inc(bn_ready, 1)
            root(0)
            root(1)
            act.wait_ge(bn_step, 6)
            act.wait_ge(c_loaded, CONSTS * DMA)
            with act.Fori(0, B - 1) as b:
                slots(act, b, slot, False)
                act.wait_ge(out_ready, (b + 1) * ROWS)
                act.wait_ge(qsum_ready, (b + 1) * ROWS)
                root(2 * b + 3)
            slots(act, B - 1, slot, True)

        @block.vector
        def _(dve):
            def flat(ap):
                return ap.rearrange("p o n -> p (o n)")

            def step(n, k, ins):
                ins.then_inc(gn_step, 1)
                dve.wait_ge(gn_step, 8 * n + k)

            def group_norm_start(n, stats, dst):
                for kt in range(KT):
                    last = nc.vector.bn_aggr(mv[:, kt, :], stats[:, kt, :, :].rearrange("p c s -> p (c s)"))
                last.then_inc(gn_in, 1)
                dve.wait_ge(gn_in, 2 * n + 1)
                dve.wait_ge(gsum_done, 2 * n + 1)
                step(n, 1, nc.vector.tensor_copy(dst[:, 0, :], ps[:, BANK_Q, 0:KT]))
                step(n, 2, nc.vector.tensor_tensor(dev[:, 0, :], mv[:, :, 0], dst[:, 0, :], ALU.subtract))
                step(n, 3, nc.vector.tensor_tensor(dev[:, 7, :], dev[:, 0, :], dev[:, 0, :], ALU.mult))
                nc.vector.tensor_tensor(dev[:, 1, :], dev[:, 7, :], mv[:, :, 1], ALU.add).then_inc(gn_in, 1)
                dve.wait_ge(gsum_done, 2 * n + 2)
                nc.vector.tensor_scalar(dev[:, 2, :], ps[:, BANK_Q, KT:2 * KT], GN_EPS, None,
                                        ALU.add).then_inc(gn_var, 1)

            def group_norm_end(n, dst):
                dve.wait_ge(gn_var, n + 1)
                dve.wait_ge(root_ready, n + 1)
                step(n, 4, nc.vector.reciprocal(dev[:, 4, :], dev[:, 3, :]))
                step(n, 5, nc.vector.tensor_tensor(dev[:, 5, :], dev[:, 4, :], dev[:, 2, :], ALU.mult))
                step(n, 6, nc.vector.tensor_tensor(dev[:, 6, :], dev[:, 5, :], dev[:, 3, :], ALU.add))
                step(n, 7, nc.vector.tensor_scalar(dev[:, 7, :], dev[:, 6, :], 0.5, None, ALU.mult))
                step(n, 8, nc.vector.reciprocal(dst[:, 1, :], dev[:, 7, :]))

            def stats_x(par, c):
                for kt in range(KT):
                    last = nc.vector.bn_stats(st0[:, kt, bass.ds(c, 1), :].rearrange("p o s -> p (o s)"),
                                              flat(xs[:, bass.ds(par, 1), kt, bass.ds(c * CHUNK, CHUNK)]))
                return last

            def fill_xp(img, par):
                for kt in range(KT):
                    last = nc.vector.tensor_scalar(
                        xp[:, kt, 1:H + 1, 1:W + 1],
                        xs[:, bass.ds(par, 1), kt, :].rearrange("p o (y x) -> p (o y) x", x=W),
                        gn0[:, 0, kt:kt + 1], gn0[:, 1, kt:kt + 1], ALU.subtract, ALU.mult)
                last.then_inc(xp_ready, 1)

            def conv(img):
                par = img % 2
                with dve.Fori(0, CHUNKS) as c:
                    for mt in range(MT):
                        n = (img * CHUNKS + c) * MT + mt
                        dve.wait_ge(conv_done, n + 1)
                        dst = flat(xs[:, bass.ds(par, 1), mt, bass.ds(c * CHUNK, CHUNK)])
                        nc.vector.tensor_tensor(dst, dst, ps[:, BANK_C[mt], 0:CHUNK], ALU.add).then_inc(conv_added, 1)
                        dve.wait_ge(conv_added, n + 3)
                        nc.vector.bn_stats(st1[:, mt, bass.ds(c, 1), :].rearrange("p o s -> p (o s)"), dst).then_inc(st1_done, 1)
                dve.wait_ge(st1_done, alone(dve, (img + 1) * (CHUNKS * MT)))

            def normalize_row(b, row, rp):
                for kt in range(KT):
                    src = xs[:, bass.ds(b % 2, 1), kt, bass.ds(row * ROW_TOK, ROW_TOK)]
                    last = nc.vector.tensor_scalar(
                        xh[:, rp, kt, :].rearrange("p (w r c) -> p w r c", r=WS, c=WS),
                        src.rearrange("p o (r w c) -> p (o w) r c", r=WS, c=WS),
                        gn1[:, 0, kt:kt + 1], gn1[:, 1, kt:kt + 1], ALU.subtract, ALU.mult)
                last.then_inc(xh_ready, 1)

            def slot(T, R0, i, b, c, last_image):
                par1 = (i + 1) % 2
                if i == -1:
                    normalize_row(b, 0, 0)
                if i + 1 < TILES:
                    dve.wait_ge(raw_ready, T + 2)
                    if i >= 1:
                        dve.wait_ge(ktv_done, 2 * T - 1)
                    nc.vector.tensor_scalar(kr[:, par1, 0:C], raw[:, par1, 0:C], 0.0, None, ALU.max).then_inc(k_ready, 1)
                if i % 2 == 0 and (i + 2) // 2 < ROWS:
                    r = (i + 2) // 2
                    if i >= 2:
                        dve.wait_ge(kv_done, T)
                        dve.wait_ge(q_done, grow(R0, i, r) - 1)
                    normalize_row(b, lrow(c, i, r), r % 2)
                if 1 <= i <= TILES:
                    for n, (w0, nw) in enumerate(BATCHES):
                        dve.wait_ge(att_done, 3 * T + (n - 2))
                        o = ps[:, BANK_O[n], 0:nw * KVW].rearrange("p (w h m) -> p w h m", w=nw, m=DIM + 1)
                        nc.vector.tensor_scalar(den[:, w0:w0 + nw, :], o[:, :, :, DIM], DEN_EPS, None,
                                                ALU.add).then_inc(den_ready, 1)
                        dve.wait_ge(den_ready, 3 * T + (n - 2))
                        nc.vector.reciprocal(rcp[:, w0:w0 + nw, :], den[:, w0:w0 + nw, :]).then_inc(rcp_ready, 1)
                        dve.wait_ge(rcp_ready, 3 * T + (n - 2))
                        if i >= 2 and n == 0:
                            dve.wait_ge(tr_done, 2 * T - 2)
                        nc.vector.tensor_tensor(
                            ao[:, w0:w0 + nw, :].rearrange("p w (h m) -> p w h m", m=DIM), o[:, :, :, 0:DIM],
                            rcp[:, w0:w0 + nw, :].unsqueeze(3).to_broadcast([P, nw, HEADS_G, DIM]),
                            ALU.mult).then_inc(ao_ready, 1)
                if 0 <= i < TILES:
                    for h in range(2):
                        dve.wait_ge(ktv_done, 2 * T + (h + 1))
                        if i >= 1:
                            for e in PLACE:
                                dve.wait_ge(placed[e], len(PLACE[e]) * T)
                        kv = ps[:, BANK_S[h], :]
                        nc.vector.tensor_tensor(
                            kvm[:, h, :, :, :].rearrange("p g s (i m) -> p (g s) i m", m=DIM + 1)[:, :, :, 0:DIM],
                            kv.rearrange("p (s i m) -> p s i m", i=HEADS_Q, m=DIM),
                            hm[:].unsqueeze(1).unsqueeze(3).to_broadcast([P, 2 * SLOTS, HEADS_Q, DIM]), ALU.mult)
                        nc.vector.tensor_tensor(
                            kvm[:, h, :, 0:NWIN, :].rearrange("p g s (i m) -> p g s i m", m=DIM + 1)[:, :, :, :, DIM],
                            kv.rearrange("p (g s) -> p g s", g=2)[:, :, NWIN * 32:NWIN * 32 + NWIN]
                            .unsqueeze(3).to_broadcast([P, 2, NWIN, HEADS_Q]),
                            hm[:].unsqueeze(1).unsqueeze(1).to_broadcast([P, 2, NWIN, HEADS_Q]),
                            ALU.mult).then_inc(masked, 1)
                    for h, q in PLACE["dve"]:
                        dve.wait_ge(masked, 2 * T + (h + 1))
                        if i >= 1:
                            dve.wait_ge(att_done, 3 * T)
                        s = slice(32 * q, 32 * q + 32)
                        nc.vector.tensor_copy(kvb[s, 2 * h:2 * h + 2, :, q * QW:(q + 1) * QW],
                                              kvm[s, h, :, 0:NWIN, :]).then_inc(placed["dve"], 1)
                if i % 2 == 0 and i < TILES:
                    r = i // 2
                    dve.wait_ge(qsum_ready, grow(R0, i, r) + 1)
                    if i >= 4:
                        dve.wait_ge(att_done, 3 * T - 6)
                    nc.vector.tensor_scalar(qs[:, MT:G, r % 2, 0:ROW_TOK],
                                            qsum[:].rearrange("p (m n) -> p m n", m=MT),
                                            POOL_SCALE, 0.0, ALU.mult, ALU.max).then_inc(qp_ready, 1)
                if not last_image:
                    if i % 4 == 1 and i < TILES:
                        if i == 1:
                            dve.wait_ge(x_loaded, (b + 2) * (KT * DMA))
                        stats_x((b + 1) % 2, c).then_inc(st0_done, 1)
                    if i == TILES - 1:
                        dve.wait_ge(st0_done, alone(dve, (b + 1) * CHUNKS))
                        group_norm_start(2 * b + 2, st0, gn0)
                    if i == TILES:
                        group_norm_end(2 * b + 2, gn0)
                        fill_xp(b + 1, (b + 1) % 2)

            nc.vector.memset(kvb[:], 0.0).then_inc(set_up, 1)
            nc.vector.memset(qs[:, :, :, ROW_TOK:], 0.0).then_inc(set_up, 1)
            dve.wait_ge(set_up, 2)
            dve.wait_ge(c_loaded, CONSTS * DMA)
            nc.vector.tensor_scalar(bnt[:, 0, :], bnp[:, 3, :], BN_EPS, None, ALU.add).then_inc(bn_step, 1)
            dve.wait_ge(bn_step, 1)
            dve.wait_ge(bn_ready, 1)
            nc.vector.reciprocal(bnt[:, 2, :], bnt[:, 1, :]).then_inc(bn_step, 1)
            dve.wait_ge(bn_step, 2)
            nc.vector.tensor_tensor(bnt[:, 3, :], bnt[:, 2, :], bnt[:, 0, :], ALU.mult).then_inc(bn_step, 1)
            dve.wait_ge(bn_step, 3)
            nc.vector.tensor_tensor(bnt[:, 4, :], bnt[:, 3, :], bnt[:, 1, :], ALU.add).then_inc(bn_step, 1)
            dve.wait_ge(bn_step, 4)
            nc.vector.tensor_scalar(bnt[:, 5, :], bnt[:, 4, :], 0.5, None, ALU.mult).then_inc(bn_step, 1)
            dve.wait_ge(bn_step, 5)
            nc.vector.reciprocal(bnt[:, 2, :], bnt[:, 5, :]).then_inc(bn_step, 1)
            dve.wait_ge(bn_step, 6)
            nc.vector.tensor_tensor(bni[:], bnp[:, 0, :], bnt[:, 2, :], ALU.mult).then_inc(bn_step, 1)
            dve.wait_ge(bn_step, 7)
            nc.vector.tensor_tensor(bnt[:, 3, :], bnp[:, 2, :], bni[:], ALU.mult).then_inc(bn_step, 1)
            dve.wait_ge(bn_step, 8)
            nc.vector.tensor_tensor(bns[:], bnp[:, 1, :], bnt[:, 3, :], ALU.subtract).then_inc(bn_step, 1)

            nc.vector.memset(dev[:, 0, :], 0.0).then_inc(conv_added, 1)
            nc.vector.memset(dev[:, 1, :], 0.0).then_inc(conv_added, 1)
            dve.wait_ge(x_loaded, KT * DMA)
            for c in range(CHUNKS):
                stats_x(0, c).then_inc(st0_done, 1)
            dve.wait_ge(st0_done, CHUNKS)
            dve.wait_ge(conv_added, 2)
            group_norm_start(0, st0, gn0)
            group_norm_end(0, gn0)
            dve.wait_ge(pad_ready, 4)
            fill_xp(0, 0)
            conv(0)
            group_norm_start(1, st1, gn1)
            group_norm_end(1, gn1)
            with dve.Fori(0, B - 1) as b:
                slots(dve, b, slot, False)
                conv(b + 1)
                group_norm_start(2 * b + 3, st1, gn1)
                group_norm_end(2 * b + 3, gn1)
            slots(dve, B - 1, slot, True)

        @block.gpsimd
        def _(pool):
            def slot(T, R0, i, b, c, last_image):
                if 0 <= i < TILES:
                    if i % 2 == 0:
                        pool.wait_ge(qsum_ready, alone(pool, grow(R0, i, i // 2) + 1))
                    elif i >= 5:
                        pool.wait_ge(out_ready, alone(pool, grow(R0, i, (i - 5) // 2) + 1))
                    for h, q in PLACE["pool"]:
                        pool.wait_ge(masked, alone(pool, 2 * T + (h + 1)))
                        if i >= 1:
                            pool.wait_ge(att_done, alone(pool, 3 * T))
                        s = slice(32 * q, 32 * q + 32)
                        nc.gpsimd.tensor_scalar(kvb[s, 2 * h:2 * h + 2, :, q * QW:(q + 1) * QW],
                                                kvm[s, h, :, 0:NWIN, :], 1.0, 0.0,
                                                ALU.mult, ALU.add).then_inc(placed["pool"], 1)
                if i % 2 == 1 and i + 1 < TILES:
                    r = (i + 1) // 2
                    n = grow(R0, i, r)
                    if i >= 1:
                        pool.wait_ge(placed["pool"], N_POOL * (T + 1))
                    pool.wait_ge(qraw_ready, n + 1)
                    col = qraw[:].rearrange("p (a c) -> p a c", c=WS)
                    hcol = qh[:].rearrange("p (a c) -> p a c", c=WS)
                    nc.gpsimd.tensor_tensor(qm[:], col[:, :, 1], col[:, :, 2], ALU.add).then_inc(q_step, 1)
                    pool.wait_ge(q_step, 6 * n + 1)
                    nc.gpsimd.tensor_tensor(hcol[:, :, 3], qm[:], col[:, :, 3], ALU.add)
                    nc.gpsimd.tensor_tensor(hcol[:, :, 0], qm[:], col[:, :, 0], ALU.add).then_inc(q_step, 1)
                    pool.wait_ge(q_step, 6 * n + 2)
                    nc.gpsimd.tensor_tensor(hcol[:, :, 1:3], hcol[:, :, 0:1].to_broadcast([P, MT * ROW_TOK // 4, 2]),
                                            col[:, :, 3:4].to_broadcast([P, MT * ROW_TOK // 4, 2]),
                                            ALU.add).then_inc(q_step, 1)
                    pool.wait_ge(q_step, 6 * n + 3)
                    row = qh[:].rearrange("p (a r c) -> p a r c", r=WS, c=WS)
                    srow = qsum[:].rearrange("p (a r c) -> p a r c", r=WS, c=WS)
                    mid = qm[:].rearrange("p (a c) -> p a c", c=WS)
                    nc.gpsimd.tensor_tensor(mid, row[:, :, 1, :], row[:, :, 2, :], ALU.add).then_inc(q_step, 1)
                    pool.wait_ge(q_step, 6 * n + 4)
                    if i >= 1:
                        pool.wait_ge(qp_ready, n)
                    nc.gpsimd.tensor_tensor(srow[:, :, 3, :], mid, row[:, :, 3, :], ALU.add).then_inc(q_step, 1)
                    nc.gpsimd.tensor_tensor(srow[:, :, 0, :], mid, row[:, :, 0, :], ALU.add).then_inc(q_step, 1)
                    pool.wait_ge(q_step, 6 * n + 6)
                    nc.gpsimd.tensor_tensor(srow[:, :, 1:3, :],
                                            srow[:, :, 0:1, :].to_broadcast([P, MT * WIN_PER_ROW, 2, WS]),
                                            row[:, :, 3:4, :].to_broadcast([P, MT * WIN_PER_ROW, 2, WS]),
                                            ALU.add).then_inc(qsum_ready, 1)
                if i % 2 == 0 and 0 <= (i - 4) // 2 < ROWS:
                    r = (i - 4) // 2
                    pool.wait_ge(y_ready, grow(R0, i, r) + 1)
                    if i < TILES:
                        pool.wait_ge(placed["pool"], N_POOL * (T + 1))
                    for mt in range(MT):
                        xrow = xs_row(b % 2, mt, lrow(c, i, r)) \
                            .rearrange("p o (r w c) -> p (o w) r c", r=WS, c=WS)
                        last = nc.gpsimd.tensor_tensor(
                            xrow, yb[:, mt, :].rearrange("p (w r c) -> p w r c", r=WS, c=WS), xrow, ALU.add)
                    last.then_inc(out_ready, 1)

            for dst in (xp[:, :, 0, :], xp[:, :, H + 1, :], xp[:, :, 1:H + 1, 0], xp[:, :, 1:H + 1, W + 1]):
                nc.gpsimd.memset(dst, 0.0).then_inc(pad_ready, 1)
            with pool.Fori(0, B) as b:
                slots(pool, b, slot, False)


def kernel(x, L0_conv_weight, L1_conv_qkv_w, L1_conv_proj_w, L1_conv_bn_gamma, L1_conv_bn_beta,
           L1_conv_bn_mean, L1_conv_bn_var):
    import concourse.bacc as bacc
    from concourse.bass_utils import run_bass_kernel_spmd

    def channels_first(w, split):
        return np.ascontiguousarray(w.reshape((split, P) + w.shape[1:]).swapaxes(0, 1))

    conv = channels_first(np.asarray(L0_conv_weight).reshape(C, C, TAPS).transpose(1, 2, 0), KT)
    heads = np.asarray(L1_conv_qkv_w).reshape(C // DIM, 3, DIM, C).transpose(3, 1, 0, 2).reshape(C, 3 * C)
    qkv = channels_first(heads, KT)
    proj = channels_first(np.asarray(L1_conv_proj_w).T, G)
    bn = np.stack([np.asarray(v).reshape(MT, P).T for v in
                   (L1_conv_bn_gamma, L1_conv_bn_beta, L1_conv_bn_mean, L1_conv_bn_var)], axis=1)

    chan = np.arange(P)
    gavg = (chan[:, None] // GN_GROUP == chan[None, :] // GN_GROUP).astype(np.float32) / GN_GROUP
    tok = np.arange(TT)
    y, xx = tok % TOK // WS, tok % WS
    pool_m = ((tok[:, None] // TOK == tok[None, :] // TOK) & (abs(y[:, None] - y[None, :]) <= 2)
              & (abs(xx[:, None] - xx[None, :]) <= 2)).astype(np.float32)
    hmask = (chan[:, None] % 32 // DIM == np.arange(HEADS_Q)[None, :]).astype(np.float32)
    vinit = np.zeros((TT, SLOTS, 2 * C // 32, 32), np.float32)
    vinit[tok, NWIN, :, tok // TOK] = 1.0

    arrays = {
        "x": np.asarray(x).reshape(B, C, HW), "w_conv": conv,
        "w_q": np.ascontiguousarray(qkv[:, :, 0:C]), "w_kv": np.ascontiguousarray(qkv[:, :, C:]),
        "w_proj": proj, "bn": np.ascontiguousarray(bn), "gavg": gavg, "pool_m": pool_m,
        "ident": np.eye(P, dtype=np.float32), "hmask": hmask, "vinit": vinit.reshape(TT, SLOTS, 2, C),
    }
    nc = bacc.Bacc("TRN2", target_bir_lowering=False, num_devices=1)
    args = [nc.dram_tensor(n, a.shape, F32, kind="ExternalInput").ap() for n, a in arrays.items()]
    out = nc.dram_tensor("out", (B, C, H, W), F32, kind="ExternalOutput").ap()
    build(nc, *args, out.rearrange("b c h w -> b c (h w)"))
    r = run_bass_kernel_spmd(nc, [arrays], core_ids=[0])
    return r.results[0]["out"]
```

```python
import numpy as np

import concourse.bass as bass
from concourse import mybir
from contextlib import ExitStack

F32 = mybir.dt.float32
F32R = mybir.dt.float32r
ALU = mybir.AluOpType
ACT = mybir.ActivationFunctionType

B, C, H, W = 8, 256, 56, 56
P = 128
KT = C // P
MT = C // P
HW = H * W
TAPS = 3
PADW = W + 2
PRODUCTS = (1, 2, 0, 3)
PARTS = ((0, 0), (0, 1), (1, 0))
PAIRS = W // 2
CONV_H = 14
CONV_CHUNKS = H // CONV_H
CONV_IN = CONV_H + 2
CONV_N = CONV_H * PAIRS
CONV_D = KT * CONV_IN * PAIRS
CONV_STEPS = CONV_CHUNKS * len(PRODUCTS)
XP_STEPS = 2 * CONV_CHUNKS - 1
TAPS_K = KT * TAPS * C
WS = 4
TOK = WS * WS
WIN_PER_ROW = W // WS
ROWS = H // WS
ROW_TOK = WIN_PER_ROW * TOK
NWIN = WIN_PER_ROW // 2
TT = NWIN * TOK
TILES = 2 * ROWS
CHUNKS = TILES // 4
CHUNK = HW // CHUNKS
DIM = 8
G = 2 * C // P
HEADS_G = P // DIM
QUADS = P // 32
HEADS_Q = 32 // DIM
KVW = QUADS * HEADS_Q * (DIM + 1)
QW = HEADS_Q * (DIM + 1)
SLOTS = NWIN + 1
GN_GROUP = C // 32
GN_EPS = 1e-5
BN_EPS = 1e-5
DEN_EPS = 1e-15
POOL_SCALE = 1.0 / 25.0
BATCHES = ((0, 3), (3, 2), (5, 2))
T_A = 4
HEAD = (ROWS - 2) * ROW_TOK
DMA = 16

CONSTS = 9

BANK_Q = 0
BANK_TA = 1
BANK_KV = 2
BANK_S = (3, 4)
BANK_O = (5, 6, 7)
BANK_TB = 7
BANK_C = ((5, 6), (3, 4))

PLACE = {"act": ((0, 0), (0, 1), (1, 0)), "pool": ((0, 2), (0, 3)), "dve": ((1, 1), (1, 2), (1, 3))}


def build(nc, x, w_conv, w_q, w_kv, w_proj, bn, gavg, pool_m, ident, hmask, vinit, out):
    ctx = ExitStack()
    with ctx:
        def sb(name, shape, dtype=F32):
            return ctx.enter_context(nc.sbuf_tensor(name, shape, dtype))

        def sem(name):
            return ctx.enter_context(nc.semaphore(name))

        wc = sb("wc", [P, 2, 4, KT * TAPS, C], F32R)
        wq = sb("wq", [P, KT, C])
        wkv = sb("wkv", [P, KT, 2 * C])
        wp = sb("wp", [P, G, C])
        bnp = sb("bnp", [P, 4, MT])
        gav = sb("gav", [P, P])
        poolm = sb("poolm", [TT, TT])
        idn = sb("idn", [P, P])
        hm = sb("hm", [P, HEADS_Q])
        xs = sb("xs", [P, 2, KT, HW])
        xp = sb("xp", [P, KT, CONV_IN, PADW])
        dp = sb("dp", [P, 2, 2, CONV_D], F32R)
        st0 = sb("st0", [P, KT, CHUNKS, 6])
        st1 = sb("st1", [P, KT, 2 * CONV_CHUNKS, 6])
        mv = sb("mv", [P, KT, 2])
        dev = sb("dev", [P, 8, KT])
        gn0 = sb("gn0", [P, 2, KT])
        gn1 = sb("gn1", [P, 2, KT])
        bni = sb("bni", [P, MT])
        bns = sb("bns", [P, MT])
        bnt = sb("bnt", [P, 6, MT])
        xh = sb("xh", [P, 2, KT, ROW_TOK])
        qs = sb("qs", [P, G, 2, ROW_TOK + TOK])
        qraw = sb("qraw", [P, MT * ROW_TOK])
        qh = sb("qh", [P, MT * ROW_TOK])
        qm = sb("qm", [P, MT * ROW_TOK // 4])
        qsum = sb("qsum", [P, MT * ROW_TOK])
        raw = sb("raw", [TT, 2, 3 * C])
        kr = sb("kr", [TT, 2, 2 * C])
        ve = sb("ve", [TT, SLOTS, 2, C])
        kvm = sb("kvm", [P, 2, 2, SLOTS, QW])
        kvb = sb("kvb", [P, G, NWIN, KVW])
        den = sb("den", [P, NWIN, HEADS_G])
        rcp = sb("rcp", [P, NWIN, HEADS_G])
        ao = sb("ao", [P, NWIN, P])
        at = sb("at", [P, G, 2, ROW_TOK])
        yb = sb("yb", [P, MT, ROW_TOK])

        ps = ctx.enter_context(nc.psum_tensor("ps", [P, 8, 512], F32))

        dt = (xh[:].rearrange("p a k n -> p (a k n)"), ao[:].rearrange("p w n -> p (w n)"))
        wspace = xs[:, 1].rearrange("p k n -> p (k n)")
        wraw = wspace[:, 0:TAPS * TAPS_K].rearrange("p (a x o) -> p a x o", x=TAPS, o=C)
        wsum = wspace[:, TAPS * TAPS_K:(TAPS + 1) * TAPS_K].rearrange("p (a o) -> p a o", o=C)
        wouter = xp[:].rearrange("p k y x -> p (k y x)")[:, 0:TAPS_K].rearrange("p (a o) -> p a o", o=C)
        wprod = (wraw[:, :, 0, :], wsum, wraw[:, :, 1, :], wraw[:, :, 2, :])

        x_loaded = sem("x_loaded")
        x_tail_loaded = sem("x_tail_loaded")
        w_loaded = sem("w_loaded")
        c_loaded = sem("c_loaded")
        ve_loaded = sem("ve_loaded")
        stored = sem("stored")
        conv_done = sem("conv_done")
        gsum_done = sem("gsum_done")
        kv_done = sem("kv_done")
        pool_done = sem("pool_done")
        q_done = sem("q_done")
        ktv_done = sem("ktv_done")
        att_done = sem("att_done")
        tr_done = sem("tr_done")
        proj_done = sem("proj_done")
        raw_ready = sem("raw_ready")
        kp_ready = sem("kp_ready")
        vp_ready = sem("vp_ready")
        placed = {e: sem("placed_" + e) for e in PLACE}
        q_ready = sem("q_ready")
        qraw_ready = sem("qraw_ready")
        at_ready = sem("at_ready")
        y_ready = sem("y_ready")
        w_high = sem("w_high")
        d_high = sem("d_high")
        root_ready = sem("root_ready")
        set_up = sem("set_up")
        conv_added = sem("conv_added")
        w_step = sem("w_step")
        w_ready = sem("w_ready")
        xp_ready = sem("xp_ready")
        d_ready = sem("d_ready")
        d_low = sem("d_low")
        gn_in = sem("gn_in")
        gn_step = sem("gn_step")
        gn_var = sem("gn_var")
        st0_done = sem("st0_done")
        st1_done = sem("st1_done")
        bn_ready = sem("bn_ready")
        bn_step = sem("bn_step")
        xh_ready = sem("xh_ready")
        k_ready = sem("k_ready")
        masked = sem("masked")
        den_ready = sem("den_ready")
        rcp_ready = sem("rcp_ready")
        ao_ready = sem("ao_ready")
        qp_ready = sem("qp_ready")
        q_step = sem("q_step")
        qsum_ready = sem("qsum_ready")
        out_ready = sem("out_ready")

        block = ctx.enter_context(nc.Block())

        N_ACT, N_POOL, N_DVE = (len(PLACE[e]) for e in ("act", "pool", "dve"))

        def first_slots(b, slot, last):
            slot(b * TILES - 1, b * ROWS, -1, b, 0, last)
            for t in range(4):
                slot(b * TILES + t, b * ROWS, t, b, 0, last)

        def later_slots(eng, b, slot, last):
            with eng.Fori(1, CHUNKS - 1) as c:
                for t in range(4):
                    slot(b * TILES + c * 4 + t, b * ROWS + c * 2, 4 + t, b, c, last)
            for i in range(TILES - 4, TILES + 1):
                slot(b * TILES + i, b * ROWS + (i // 4) * 2, i, b, i // 4, last)

        def slots(eng, b, slot, last):
            first_slots(b, slot, last)
            later_slots(eng, b, slot, last)

        def grow(R0, i, r):
            return R0 + (r - (2 * (i // 4) if i >= 0 else 0))

        def lrow(c, i, r):
            return c * 2 + (r - (2 * (i // 4) if i >= 0 else 0))

        def xs_row(par, mt, row, n=ROW_TOK):
            return xs[:, bass.ds(par, 1), mt, bass.ds(row * ROW_TOK, n)]

        def alone(eng, value):
            value = value if isinstance(value, int) else eng.to_reg(value)
            eng.wait_ge(c_loaded, DMA)
            return value

        @block.sync
        def _(sp):
            def load_x(img, part):
                lo, hi, loaded = ((0, HEAD, x_loaded), (HEAD, HW, x_tail_loaded))[part]
                for kt in range(KT):
                    sp.dma_start(xs[:, bass.ds(img % 2, 1), kt, lo:hi],
                                 x[bass.ds(img, 1), kt * P:(kt + 1) * P, lo:hi].rearrange("o p n -> p o n")).then_inc(loaded, DMA)

            def store_row(b, n, row):
                sp.wait_ge(out_ready, alone(sp, n + 1))
                for mt in range(MT):
                    sp.dma_start(out[bass.ds(b, 1), mt * P:(mt + 1) * P, bass.ds(row * ROW_TOK, ROW_TOK)]
                                 .rearrange("o p n -> p o n"),
                                 xs_row(b % 2, mt, row)).then_inc(stored, DMA)

            sp.dma_start(wspace[:, 0:TAPS * TAPS_K], w_conv).then_inc(w_loaded, DMA)
            load_x(0, 0)
            load_x(0, 1)
            for dst, src in ((gav, gavg), (bnp, bn)):
                sp.dma_start(dst[:], src).then_inc(c_loaded, DMA)
            for dst, src in ((wq, w_q), (wkv, w_kv), (wp, w_proj), (poolm, pool_m), (idn, ident), (hm, hmask)):
                sp.dma_start(dst[:], src).then_inc(c_loaded, DMA)
            sp.dma_start(ve[:], vinit).then_inc(c_loaded, DMA)
            sp.wait_ge(c_loaded, CONSTS * DMA)
            sp.wait_ge(x_loaded, KT * DMA)
            sp.wait_ge(x_tail_loaded, KT * DMA)
            sp.wait_ge(w_ready, len(PRODUCTS))
            load_x(1, 0)
            load_x(1, 1)

            def slot(T, R0, i, b, c, last):
                if i + 1 < TILES:
                    par = (i + 1) % 2
                    sp.wait_ge(vp_ready, alone(sp, T + 2))
                    if i >= 0:
                        sp.wait_ge(ktv_done, alone(sp, 2 * T + 2))
                    for w in range(NWIN):
                        sp.dma_start(ve[w * TOK:(w + 1) * TOK, w].rearrange("p h c -> p (h c)"),
                                     raw[w * TOK:(w + 1) * TOK, par, C:3 * C]).then_inc(ve_loaded, DMA)
                if i % 2 == 0 and 0 <= (i - 4) // 2 < ROWS - 2:
                    r = (i - 4) // 2
                    store_row(b, grow(R0, i, r), lrow(c, i, r))

            def last_rows(b):
                for row in (ROWS - 2, ROWS - 1):
                    store_row(b, b * ROWS + row, row)

            first_slots(0, slot, False)
            with sp.Fori(0, B - 2) as b:
                later_slots(sp, b, slot, False)
                sp.wait_ge(stored, alone(sp, (b * ROWS + ROWS - 2) * (MT * DMA)))
                load_x(b + 2, 0)
                last_rows(b)
                first_slots(b + 1, slot, False)
                sp.wait_ge(stored, alone(sp, (b + 1) * (MT * ROWS * DMA)))
                load_x(b + 2, 1)
            later_slots(sp, B - 2, slot, False)
            last_rows(B - 2)
            slots(sp, B - 1, slot, True)
            last_rows(B - 1)
            sp.wait_ge(stored, B * MT * ROWS * DMA)

        @block.tensor
        def _(pe):
            def conv(img):
                with pe.Fori(0, CONV_CHUNKS) as c:
                    for kk, k in enumerate(PRODUCTS):
                        v = (img * CONV_CHUNKS + c) * len(PRODUCTS) + kk
                        pe.wait_ge(d_low, v + 1)
                        for mt in range(MT):
                            pe.wait_ge(conv_added, 2 * v + mt + 1)
                            n = 0
                            for part_w, part_d in PARTS:
                                for kt in range(KT):
                                    for dy in range(TAPS):
                                        d0 = (kt * CONV_IN + dy) * PAIRS
                                        last = nc.tensor.matmul(
                                            ps[:, BANK_C[kk % 2][mt], 0:CONV_N],
                                            wc[:, part_w, k, kt * TAPS + dy, mt * P:(mt + 1) * P],
                                            dp[:, kk % 2, part_d, d0:d0 + CONV_N],
                                            start=(n == 0), stop=(n == len(PARTS) * KT * TAPS - 1))
                                        n += 1
                            last.then_inc(conv_done, 1)

            def group_sums(n, steps=(0, 1)):
                for s in steps:
                    pe.wait_ge(gn_in, 2 * n + s + 1)
                    src = mv[:, :, 0] if s == 0 else dev[:, 1, :]
                    nc.tensor.matmul(ps[:, BANK_TA, s * KT:(s + 1) * KT], gav[:], src,
                                     start=True, stop=True).then_inc(gsum_done, 1)

            def slot(T, R0, i, b, c, last_image):
                par1, par = (i + 1) % 2, i % 2
                if i + 1 < TILES:
                    rp = ((i + 1) // 2) % 2
                    if i % 2 == 1:
                        pe.wait_ge(xh_ready, grow(R0, i, (i + 1) // 2) + 1)
                    if i >= 0:
                        pe.wait_ge(vp_ready, T + 1)
                    off = ((i + 1) % 2) * TT
                    for kt in range(KT):
                        last = nc.tensor.matmul(ps[0:TT, BANK_KV, :], xh[:, rp, kt, off:off + TT],
                                                wkv[:, kt, :], start=(kt == 0), stop=(kt == KT - 1))
                    last.then_inc(kv_done, 1)
                if 1 <= i <= TILES:
                    j = i - 1
                    rp, off = (j // 2) % 2, (j % 2) * TT
                    pe.wait_ge(placed["act"], N_ACT * T)
                    pe.wait_ge(placed["pool"], N_POOL * T)
                    pe.wait_ge(placed["dve"], N_DVE * T)
                    pe.wait_ge(q_ready, grow(R0, i, j // 2) + 1)
                    pe.wait_ge(qp_ready, grow(R0, i, j // 2) + 1)
                    for n, (w0, nw) in enumerate(BATCHES):
                        if j >= 1:
                            pe.wait_ge(ao_ready, 3 * T + (n - 5))
                            if BANK_O[n] == BANK_TB:
                                pe.wait_ge(at_ready, 2 * T - 2)
                        for w in range(w0, w0 + nw):
                            for g in range(G):
                                o = off + w * TOK
                                last = nc.tensor.matmul(
                                    ps[32 * g:32 * g + 32, BANK_O[n], (w - w0) * KVW:(w - w0 + 1) * KVW],
                                    qs[:, g, rp, o:o + 2 * TOK], kvb[:, g, w, :], start=True, stop=True)
                        last.then_inc(att_done, 1)
                if not last_image and i in (TILES - 2, TILES - 1):
                    group_sums(2 * b + 2, (i - (TILES - 2),))
                if i + 1 < TILES:
                    pe.wait_ge(raw_ready, T + 2)
                    nc.tensor.matmul(ps[0:TT, BANK_KV, :], poolm[:], raw[:, par1, 0:2 * C],
                                     start=True, stop=True).then_inc(pool_done, 1)
                if 0 <= i < TILES:
                    for h in range(2):
                        pe.wait_ge(ve_loaded, (T + 1) * (NWIN * DMA))
                        pe.wait_ge(k_ready if h == 0 else kp_ready, T + 1)
                        if i >= 1:
                            pe.wait_ge(masked, 2 * T + (h - 1))
                        for gg in range(2):
                            for q in range(QUADS):
                                k0 = h * C + gg * P + 32 * q
                                v0 = gg * P + 32 * q
                                last = nc.tensor.matmul(
                                    ps[32 * q:32 * q + 32, BANK_S[h], gg * C:(gg + 1) * C],
                                    kr[:, par, k0:k0 + 32], ve[:, :, h, v0:v0 + 32], start=True, stop=True)
                        last.then_inc(ktv_done, 1)
                if i % 2 == 1 and i + 1 < TILES:
                    r = (i + 1) // 2
                    if i >= 5:
                        pe.wait_ge(y_ready, grow(R0, i, (i - 5) // 2) + 1)
                    for mt in range(MT):
                        for kt in range(KT):
                            last = nc.tensor.matmul(ps[:, BANK_Q, mt * ROW_TOK:(mt + 1) * ROW_TOK],
                                                    wq[:, kt, mt * P:(mt + 1) * P], xh[:, r % 2, kt, :],
                                                    start=(kt == 0), stop=(kt == KT - 1))
                    last.then_inc(q_done, 1)
                if 1 <= i <= TILES:
                    for n, (w0, w1) in enumerate(((0, T_A), (T_A, NWIN))):
                        pe.wait_ge(ao_ready, 3 * T + (n - 1))
                        if n == 0 and i >= 2:
                            pe.wait_ge(at_ready, 2 * T - 3)
                        if n == 0 and not last_image and i == TILES - 2:
                            pe.wait_ge(gn_step, 8 * (2 * b + 2) + 1)
                        if n == 0 and not last_image and i == TILES - 1:
                            pe.wait_ge(gn_var, 2 * b + 3)
                        for w in range(w0, w1):
                            last = nc.tensor.transpose(ps[:, BANK_TA if n == 0 else BANK_TB, (w - w0) * P:(w - w0 + 1) * P],
                                                       ao[:, w, :], idn[:])
                        last.then_inc(tr_done, 1)
                if i % 2 == 0 and 0 <= (i - 4) // 2 < ROWS - 2:
                    r = (i - 4) // 2
                    pe.wait_ge(at_ready, 2 * T - 4)
                    if i < TILES:
                        pe.wait_ge(q_ready, grow(R0, i, i // 2) + 1)
                        pe.wait_ge(qraw_ready, grow(R0, i, i // 2) + 1)
                    project(r % 2)

            def project(rp):
                for mt in range(MT):
                    for g in range(G):
                        last = nc.tensor.matmul(ps[:, BANK_Q, mt * ROW_TOK:(mt + 1) * ROW_TOK],
                                                wp[:, g, mt * P:(mt + 1) * P], at[:, g, rp, :],
                                                start=(g == 0), stop=(g == G - 1))
                last.then_inc(proj_done, 1)

            def last_row(b, row):
                pe.wait_ge(at_ready, (b + 1) * (2 * TILES))
                pe.wait_ge(y_ready, b * ROWS + row)
                project(row % 2)

            pe.wait_ge(c_loaded, CONSTS * DMA)
            group_sums(0)
            pe.wait_ge(w_ready, len(PRODUCTS))
            conv(0)
            group_sums(1)
            with pe.Fori(0, B - 1) as b:
                slots(pe, b, slot, False)
                conv(b + 1)
                last_row(b, ROWS - 2)
                group_sums(2 * b + 3)
                last_row(b, ROWS - 1)
                pe.wait_ge(y_ready, (b + 1) * ROWS)
            slots(pe, B - 1, slot, True)
            last_row(B - 1, ROWS - 2)
            last_row(B - 1, ROWS - 1)

        @block.scalar
        def _(act):
            def root(n):
                act.wait_ge(gn_var, n + 1)
                nc.scalar.activation(dev[:, 3, :], dev[:, 2, :], ACT.Sqrt).then_inc(root_ready, 1)

            def split(v, kk, first=False):
                act.wait_ge(d_ready, v + 1)
                if not first:
                    act.wait_ge(conv_done, 2 * v - 2)
                nc.scalar.copy(dp[:, kk % 2, 0, :], dt[kk % 2]).then_inc(d_high, 1)

            def split_rest(img):
                with act.Fori(0, CONV_CHUNKS - 1) as c:
                    for kk in range(4):
                        split(img * CONV_STEPS + c * 4 + 2 + kk, kk)
                for kk in (2, 3):
                    split(img * CONV_STEPS + CONV_STEPS - 4 + kk, kk)

            def slot(T, R0, i, b, c, last_image):
                par1 = (i + 1) % 2
                if i + 1 < TILES:
                    act.wait_ge(kv_done, T + 2)
                    if i >= 1:
                        act.wait_ge(pool_done, T)
                        act.wait_ge(k_ready, T)
                        act.wait_ge(ve_loaded, T * (NWIN * DMA))
                    nc.scalar.copy(raw[:, par1, 0:2 * C], ps[0:TT, BANK_KV, :]).then_inc(raw_ready, 1)
                    act.wait_ge(pool_done, T + 2)
                    if i >= 1:
                        act.wait_ge(ktv_done, 2 * T)
                    nc.scalar.activation(kr[:, par1, C:2 * C], ps[0:TT, BANK_KV, 0:C], ACT.Relu,
                                         scale=POOL_SCALE).then_inc(kp_ready, 1)
                    nc.scalar.activation(raw[:, par1, 2 * C:3 * C], ps[0:TT, BANK_KV, C:2 * C], ACT.Copy,
                                         scale=POOL_SCALE).then_inc(vp_ready, 1)
                if 0 <= i < TILES:
                    for h, q in PLACE["act"]:
                        act.wait_ge(masked, 2 * T + (h + 1))
                        if i >= 1:
                            act.wait_ge(att_done, 3 * T)
                        s = slice(32 * q, 32 * q + 32)
                        nc.scalar.copy(kvb[s, 2 * h:2 * h + 2, :, q * QW:(q + 1) * QW],
                                       kvm[s, h, :, 0:NWIN, :]).then_inc(placed["act"], 1)
                if i % 2 == 1 and i + 1 < TILES:
                    r = (i + 1) // 2
                    act.wait_ge(q_done, grow(R0, i, r) + 1)
                    if i >= 3:
                        act.wait_ge(att_done, 3 * T - 3)
                    nc.scalar.activation(qs[:, 0:MT, r % 2, 0:ROW_TOK],
                                         ps[:, BANK_Q, 0:MT * ROW_TOK].rearrange("p (m n) -> p m n", m=MT),
                                         ACT.Relu).then_inc(q_ready, 1)
                    if i >= 1:
                        act.wait_ge(qsum_ready, grow(R0, i, r))
                    nc.scalar.copy(qraw[:], ps[:, BANK_Q, 0:MT * ROW_TOK]).then_inc(qraw_ready, 1)
                if i == TILES and not last_image:
                    split((b + 1) * CONV_STEPS, 0)
                if 1 <= i <= TILES:
                    j = i - 1
                    rp, off = (j // 2) % 2, (j % 2) * TT
                    for n, (w0, w1) in enumerate(((0, T_A), (T_A, NWIN))):
                        act.wait_ge(tr_done, 2 * T + (n - 1))
                        src = ps[:, BANK_TA if n == 0 else BANK_TB, 0:(w1 - w0) * P]
                        nc.scalar.copy(
                            at[:, :, rp, off + w0 * TOK:off + w1 * TOK].rearrange("p g (w t) -> p w g t", t=TOK),
                            src.rearrange("p (w g t) -> p w g t", g=G, t=2 * TOK)[:, :, :, 0:TOK]).then_inc(at_ready, 1)
                if i % 2 == 0 and 0 <= (i - 4) // 2 < ROWS - 2:
                    r = (i - 4) // 2
                    batch_norm(grow(R0, i, r), first=(r == 0))
                if i == TILES - 1 and not last_image:
                    root(2 * b + 2)

            def batch_norm(n, first=False):
                act.wait_ge(proj_done, n + 1)
                if not first:
                    act.wait_ge(out_ready, n)
                for mt in range(MT):
                    last = nc.scalar.activation(yb[:, mt, :], ps[:, BANK_Q, mt * ROW_TOK:(mt + 1) * ROW_TOK],
                                                ACT.Identity, bias=bns[:, mt:mt + 1], scale=bni[:, mt:mt + 1])
                last.then_inc(y_ready, 1)

            act.wait_ge(bn_step, 1)
            nc.scalar.activation(bnt[:, 1, :], bnt[:, 0, :], ACT.Sqrt).then_inc(bn_ready, 1)
            act.wait_ge(w_loaded, DMA)
            for n, k in enumerate((0, 3, 1, 2)):
                if n >= 2:
                    act.wait_ge(w_step, n + 2)
                nc.scalar.copy(wc[:, 0, k], wprod[k]).then_inc(w_high, 1)
            root(0)
            for kk in range(2):
                split(kk, kk, first=True)
            split_rest(0)
            root(1)
            act.wait_ge(bn_step, 6)
            act.wait_ge(c_loaded, CONSTS * DMA)
            with act.Fori(0, B - 1) as b:
                slots(act, b, slot, False)
                split((b + 1) * CONV_STEPS + 1, 1)
                act.wait_ge(qsum_ready, (b + 1) * ROWS)
                split_rest(b + 1)
                batch_norm(b * ROWS + ROWS - 2)
                root(2 * b + 3)
                batch_norm(b * ROWS + ROWS - 1)
                act.wait_ge(out_ready, (b + 1) * ROWS)
            slots(act, B - 1, slot, True)
            batch_norm(B * ROWS - 2)
            batch_norm(B * ROWS - 1)

        @block.vector
        def _(dve):
            def flat(ap):
                return ap.rearrange("p o n -> p (o n)")

            def step(n, k, ins):
                ins.then_inc(gn_step, 1)
                dve.wait_ge(gn_step, 8 * n + k)

            def group_norm_start(n, stats, dst):
                channel_stats(n, stats)
                group_means(n, dst)
                group_variances(n)

            def channel_stats(n, stats):
                for kt in range(KT):
                    last = nc.vector.bn_aggr(mv[:, kt, :], stats[:, kt, :, :].rearrange("p c s -> p (c s)"))
                last.then_inc(gn_in, 1)

            def group_means(n, dst):
                dve.wait_ge(gn_in, 2 * n + 1)
                dve.wait_ge(gsum_done, 2 * n + 1)
                step(n, 1, nc.vector.tensor_copy(dst[:, 0, :], ps[:, BANK_TA, 0:KT]))
                step(n, 2, nc.vector.tensor_tensor(dev[:, 0, :], mv[:, :, 0], dst[:, 0, :], ALU.subtract))
                step(n, 3, nc.vector.tensor_tensor(dev[:, 7, :], dev[:, 0, :], dev[:, 0, :], ALU.mult))
                nc.vector.tensor_tensor(dev[:, 1, :], dev[:, 7, :], mv[:, :, 1], ALU.add).then_inc(gn_in, 1)

            def group_variances(n):
                dve.wait_ge(gsum_done, 2 * n + 2)
                nc.vector.tensor_scalar(dev[:, 2, :], ps[:, BANK_TA, KT:2 * KT], GN_EPS, None,
                                        ALU.add).then_inc(gn_var, 1)

            def group_norm_end(n, dst):
                dve.wait_ge(gn_var, n + 1)
                dve.wait_ge(root_ready, n + 1)
                step(n, 4, nc.vector.reciprocal(dev[:, 4, :], dev[:, 3, :]))
                step(n, 5, nc.vector.tensor_tensor(dev[:, 5, :], dev[:, 4, :], dev[:, 2, :], ALU.mult))
                step(n, 6, nc.vector.tensor_tensor(dev[:, 6, :], dev[:, 5, :], dev[:, 3, :], ALU.add))
                step(n, 7, nc.vector.tensor_scalar(dev[:, 7, :], dev[:, 6, :], 0.5, None, ALU.mult))
                step(n, 8, nc.vector.reciprocal(dst[:, 1, :], dev[:, 7, :]))

            def stats_x(par, c):
                for kt in range(KT):
                    last = nc.vector.bn_stats(st0[:, kt, bass.ds(c, 1), :].rearrange("p o s -> p (o s)"),
                                              flat(xs[:, bass.ds(par, 1), kt, bass.ds(c * CHUNK, CHUNK)]))
                return last

            def fill_xp(par, row, rows, to):
                for kt in range(KT):
                    last = nc.vector.tensor_scalar(
                        xp[:, kt, to:to + rows, 1:W + 1],
                        xs[:, bass.ds(par, 1), kt, bass.ds(row * W, rows * W)].rearrange("p o (y x) -> p (o y) x", x=W),
                        gn0[:, 0, kt:kt + 1], gn0[:, 1, kt:kt + 1], ALU.subtract, ALU.mult)
                return last

            def first_chunk(img, par):
                nc.vector.memset(xp[:, :, 0, :], 0.0)
                fill_xp(par, 0, CONV_IN - 1, 1).then_inc(xp_ready, 1)

            def next_chunk(img, par, c, edge):
                dve.wait_ge(d_ready, alone(dve, img * CONV_STEPS + c * 4 + 4))
                nc.vector.tensor_copy(xp[:, :, 0:2, :], xp[:, :, CONV_H:CONV_IN, :]).then_inc(xp_ready, 1)
                dve.wait_ge(xp_ready, alone(dve, img * XP_STEPS + c * 2 + 2))
                if edge:
                    nc.vector.memset(xp[:, :, CONV_IN - 1, :], 0.0)
                fill_xp(par, c * CONV_H + CONV_IN - 1, CONV_H - edge, 2).then_inc(xp_ready, 1)

            def product_inputs(img, c, kk, first=False):
                if kk == 0:
                    dve.wait_ge(xp_ready, alone(dve, img * XP_STEPS + c * 2 + 1))
                if not first:
                    dve.wait_ge(d_low, alone(dve, (img * CONV_CHUNKS + c) * 4 + kk - 1))
                d = [xp[:, :, :, j:j + W - 1:2].rearrange("p k y x -> p (k y) x") for j in range(4)]
                in0, in1, op = ((d[0], d[2], ALU.subtract), (d[1], d[2], ALU.add),
                                (d[2], d[1], ALU.subtract), (d[1], d[3], ALU.subtract))[PRODUCTS[kk]]
                nc.vector.tensor_tensor(dt[kk % 2].rearrange("p (y x) -> p y x", x=PAIRS),
                                        in0, in1, op).then_inc(d_ready, 1)

            def low_parts(v, kk):
                dve.wait_ge(d_high, v + 1)
                nc.vector.tensor_tensor(dp[:, kk % 2, 1, :], dt[kk % 2], dp[:, kk % 2, 0, :].bitcast(F32),
                                        ALU.subtract).then_inc(d_low, 1)

            def conv(img):
                par = img % 2

                def chunk(c, left):
                    for kk, k in enumerate(PRODUCTS):
                        v = (img * CONV_CHUNKS + c) * 4 + kk
                        if left or kk < 3:
                            low_parts(v + 1, (kk + 1) % 4)
                        if left and kk == 2:
                            next_chunk(img, par, c, left == 1)
                        if left or kk < 2:
                            product_inputs(img, c + (kk + 2) // 4, (kk + 2) % 4)
                        for mt in range(MT):
                            dve.wait_ge(conv_done, 2 * v + mt + 1)
                            if k != PRODUCTS[0]:
                                dve.wait_ge(conv_added, 2 * v + mt + 3)
                            pair = flat(xs[:, bass.ds(par, 1), mt, bass.ds(c * (CONV_H * W), CONV_H * W)]) \
                                .rearrange("p (n e) -> p n e", e=2)
                            for e, op in {0: ((0, ALU.add),), 1: ((0, ALU.add), (1, ALU.add)),
                                          2: ((0, ALU.add), (1, ALU.subtract)), 3: ((1, ALU.subtract),)}[k]:
                                last = nc.vector.tensor_tensor(pair[:, :, e], pair[:, :, e],
                                                               ps[:, BANK_C[kk % 2][mt], 0:CONV_N], op)
                            last.then_inc(conv_added, 1)
                            if k == PRODUCTS[-1]:
                                dve.wait_ge(conv_added, alone(dve, 2 * v + mt + 5))
                                for half in range(2):
                                    last = nc.vector.bn_stats(
                                        st1[:, mt, bass.ds(2 * c + half, 1), :].rearrange("p o s -> p (o s)"),
                                        flat(xs[:, bass.ds(par, 1), mt,
                                                bass.ds(c * (CONV_H * W) + half * CONV_N, CONV_N)]))
                                last.then_inc(st1_done, 1)

                with dve.Fori(0, CONV_CHUNKS - 2) as c:
                    chunk(c, 2)
                chunk(CONV_CHUNKS - 2, 1)
                chunk(CONV_CHUNKS - 1, 0)
                dve.wait_ge(st1_done, alone(dve, (img + 1) * (CONV_CHUNKS * MT)))

            def normalize_row(b, row, rp):
                for kt in range(KT):
                    src = xs[:, bass.ds(b % 2, 1), kt, bass.ds(row * ROW_TOK, ROW_TOK)]
                    last = nc.vector.tensor_scalar(
                        xh[:, rp, kt, :].rearrange("p (w r c) -> p w r c", r=WS, c=WS),
                        src.rearrange("p o (r w c) -> p (o w) r c", r=WS, c=WS),
                        gn1[:, 0, kt:kt + 1], gn1[:, 1, kt:kt + 1], ALU.subtract, ALU.mult)
                last.then_inc(xh_ready, 1)

            def slot(T, R0, i, b, c, last_image):
                par1 = (i + 1) % 2
                if i == -1:
                    normalize_row(b, 0, 0)
                if i + 1 < TILES:
                    dve.wait_ge(raw_ready, T + 2)
                    if i >= 1:
                        dve.wait_ge(ktv_done, 2 * T - 1)
                    nc.vector.tensor_scalar(kr[:, par1, 0:C], raw[:, par1, 0:C], 0.0, None, ALU.max).then_inc(k_ready, 1)
                if i % 2 == 0 and (i + 2) // 2 < ROWS:
                    r = (i + 2) // 2
                    if i >= 2:
                        dve.wait_ge(kv_done, T)
                        dve.wait_ge(q_done, grow(R0, i, r) - 1)
                    normalize_row(b, lrow(c, i, r), r % 2)
                if 1 <= i <= TILES:
                    for n, (w0, nw) in enumerate(BATCHES):
                        dve.wait_ge(att_done, 3 * T + (n - 2))
                        o = ps[:, BANK_O[n], 0:nw * KVW].rearrange("p (w h m) -> p w h m", w=nw, m=DIM + 1)
                        nc.vector.tensor_scalar(den[:, w0:w0 + nw, :], o[:, :, :, DIM], DEN_EPS, None,
                                                ALU.add).then_inc(den_ready, 1)
                        dve.wait_ge(den_ready, 3 * T + (n - 2))
                        nc.vector.reciprocal(rcp[:, w0:w0 + nw, :], den[:, w0:w0 + nw, :]).then_inc(rcp_ready, 1)
                        dve.wait_ge(rcp_ready, 3 * T + (n - 2))
                        if i >= 2 and n == 0:
                            dve.wait_ge(tr_done, 2 * T - 2)
                        nc.vector.tensor_tensor(
                            ao[:, w0:w0 + nw, :].rearrange("p w (h m) -> p w h m", m=DIM), o[:, :, :, 0:DIM],
                            rcp[:, w0:w0 + nw, :].unsqueeze(3).to_broadcast([P, nw, HEADS_G, DIM]),
                            ALU.mult).then_inc(ao_ready, 1)
                if i == TILES - 2 and not last_image:
                    group_means(2 * b + 2, gn0)
                if i == TILES - 1 and not last_image:
                    group_variances(2 * b + 2)
                if 0 <= i < TILES:
                    for h in range(2):
                        dve.wait_ge(ktv_done, 2 * T + (h + 1))
                        if i >= 1:
                            for e in PLACE:
                                dve.wait_ge(placed[e], len(PLACE[e]) * T)
                        kv = ps[:, BANK_S[h], :]
                        nc.vector.tensor_tensor(
                            kvm[:, h, :, :, :].rearrange("p g s (i m) -> p (g s) i m", m=DIM + 1)[:, :, :, 0:DIM],
                            kv.rearrange("p (s i m) -> p s i m", i=HEADS_Q, m=DIM),
                            hm[:].unsqueeze(1).unsqueeze(3).to_broadcast([P, 2 * SLOTS, HEADS_Q, DIM]), ALU.mult)
                        nc.vector.tensor_tensor(
                            kvm[:, h, :, 0:NWIN, :].rearrange("p g s (i m) -> p g s i m", m=DIM + 1)[:, :, :, :, DIM],
                            kv.rearrange("p (g s) -> p g s", g=2)[:, :, NWIN * 32:NWIN * 32 + NWIN]
                            .unsqueeze(3).to_broadcast([P, 2, NWIN, HEADS_Q]),
                            hm[:].unsqueeze(1).unsqueeze(1).to_broadcast([P, 2, NWIN, HEADS_Q]),
                            ALU.mult).then_inc(masked, 1)
                    for h, q in PLACE["dve"]:
                        dve.wait_ge(masked, 2 * T + (h + 1))
                        if i >= 1:
                            dve.wait_ge(att_done, 3 * T)
                        s = slice(32 * q, 32 * q + 32)
                        nc.vector.tensor_copy(kvb[s, 2 * h:2 * h + 2, :, q * QW:(q + 1) * QW],
                                              kvm[s, h, :, 0:NWIN, :]).then_inc(placed["dve"], 1)
                if i % 2 == 0 and i < TILES:
                    r = i // 2
                    dve.wait_ge(qsum_ready, grow(R0, i, r) + 1)
                    if i >= 4:
                        dve.wait_ge(att_done, 3 * T - 6)
                    nc.vector.tensor_scalar(qs[:, MT:G, r % 2, 0:ROW_TOK],
                                            qsum[:].rearrange("p (m n) -> p m n", m=MT),
                                            POOL_SCALE, 0.0, ALU.mult, ALU.max).then_inc(qp_ready, 1)
                if not last_image:
                    if (i % 4 == 1 and i < TILES - 4) or i == TILES - 4:
                        if i == 1:
                            dve.wait_ge(x_loaded, (b + 2) * (KT * DMA))
                        if i == TILES - 4:
                            dve.wait_ge(x_tail_loaded, (b + 2) * (KT * DMA))
                        stats_x((b + 1) % 2, c).then_inc(st0_done, 1)
                    if i == TILES - 4:
                        dve.wait_ge(st0_done, alone(dve, (b + 2) * CHUNKS))
                        channel_stats(2 * b + 2, st0)
                    if i == TILES - 1:
                        group_norm_end(2 * b + 2, gn0)
                        first_chunk(b + 1, (b + 1) % 2)
                        product_inputs(b + 1, 0, 0, first=True)
                    if i == TILES:
                        low_parts((b + 1) * CONV_STEPS, 0)
                        dve.wait_ge(tr_done, 2 * T)
                        product_inputs(b + 1, 0, 1, first=True)

            nc.vector.memset(kvb[:], 0.0).then_inc(set_up, 1)
            nc.vector.memset(qs[:, :, :, ROW_TOK:], 0.0).then_inc(set_up, 1)
            dve.wait_ge(set_up, 2)
            dve.wait_ge(c_loaded, CONSTS * DMA)
            nc.vector.tensor_scalar(bnt[:, 0, :], bnp[:, 3, :], BN_EPS, None, ALU.add).then_inc(bn_step, 1)
            dve.wait_ge(bn_step, 1)
            dve.wait_ge(bn_ready, 1)
            nc.vector.reciprocal(bnt[:, 2, :], bnt[:, 1, :]).then_inc(bn_step, 1)
            dve.wait_ge(bn_step, 2)
            nc.vector.tensor_tensor(bnt[:, 3, :], bnt[:, 2, :], bnt[:, 0, :], ALU.mult).then_inc(bn_step, 1)
            dve.wait_ge(bn_step, 3)
            nc.vector.tensor_tensor(bnt[:, 4, :], bnt[:, 3, :], bnt[:, 1, :], ALU.add).then_inc(bn_step, 1)
            dve.wait_ge(bn_step, 4)
            nc.vector.tensor_scalar(bnt[:, 5, :], bnt[:, 4, :], 0.5, None, ALU.mult).then_inc(bn_step, 1)
            dve.wait_ge(bn_step, 5)
            nc.vector.reciprocal(bnt[:, 2, :], bnt[:, 5, :]).then_inc(bn_step, 1)
            dve.wait_ge(bn_step, 6)
            nc.vector.tensor_tensor(bni[:], bnp[:, 0, :], bnt[:, 2, :], ALU.mult).then_inc(bn_step, 1)
            dve.wait_ge(bn_step, 7)
            nc.vector.tensor_tensor(bnt[:, 3, :], bnp[:, 2, :], bni[:], ALU.mult).then_inc(bn_step, 1)
            dve.wait_ge(bn_step, 8)
            nc.vector.tensor_tensor(bns[:], bnp[:, 1, :], bnt[:, 3, :], ALU.subtract).then_inc(bn_step, 1)

            for k in range(4):
                nc.vector.memset(dev[:, k, :], 0.0).then_inc(conv_added, 1)

            def w_do(n, ins):
                ins.then_inc(w_step, 1)
                dve.wait_ge(w_step, n)

            g0, gsum, g1, g2 = wprod
            dve.wait_ge(w_loaded, DMA)
            w_do(1, nc.vector.tensor_tensor(wouter, g0, g2, ALU.add))
            w_do(2, nc.vector.tensor_tensor(gsum, wouter, g1, ALU.add))
            w_do(3, nc.vector.tensor_scalar(gsum, gsum, 0.5, None, ALU.mult))
            w_do(4, nc.vector.tensor_tensor(g1, wouter, g1, ALU.subtract))
            w_do(5, nc.vector.tensor_scalar(g1, g1, 0.5, None, ALU.mult))
            for n, k in enumerate((0, 3, 1, 2)):
                dve.wait_ge(w_high, n + 1)
                nc.vector.tensor_tensor(wc[:, 1, k], wprod[k], wc[:, 0, k].bitcast(F32),
                                        ALU.subtract).then_inc(w_ready, 1)
            dve.wait_ge(w_ready, len(PRODUCTS))
            nc.vector.memset(xp[:], 0.0).then_inc(set_up, 1)
            dve.wait_ge(x_loaded, KT * DMA)
            for c in range(CHUNKS):
                if c == CHUNKS - 1:
                    dve.wait_ge(x_tail_loaded, KT * DMA)
                stats_x(0, c).then_inc(st0_done, 1)
            dve.wait_ge(st0_done, CHUNKS)
            dve.wait_ge(conv_added, 4)
            group_norm_start(0, st0, gn0)
            group_norm_end(0, gn0)
            dve.wait_ge(set_up, 3)
            first_chunk(0, 0)
            product_inputs(0, 0, 0, first=True)
            product_inputs(0, 0, 1, first=True)
            low_parts(0, 0)
            conv(0)
            group_norm_start(1, st1, gn1)
            group_norm_end(1, gn1)
            with dve.Fori(0, B - 1) as b:
                slots(dve, b, slot, False)
                conv(b + 1)
                group_norm_start(2 * b + 3, st1, gn1)
                group_norm_end(2 * b + 3, gn1)
            slots(dve, B - 1, slot, True)

        @block.gpsimd
        def _(pool):
            def slot(T, R0, i, b, c, last_image):
                if 0 <= i < TILES:
                    if i % 2 == 0:
                        pool.wait_ge(qsum_ready, alone(pool, grow(R0, i, i // 2) + 1))
                    elif i >= 5:
                        pool.wait_ge(out_ready, alone(pool, grow(R0, i, (i - 5) // 2) + 1))
                    for h, q in PLACE["pool"]:
                        pool.wait_ge(masked, alone(pool, 2 * T + (h + 1)))
                        if i >= 1:
                            pool.wait_ge(att_done, alone(pool, 3 * T))
                        s = slice(32 * q, 32 * q + 32)
                        nc.gpsimd.tensor_scalar(kvb[s, 2 * h:2 * h + 2, :, q * QW:(q + 1) * QW],
                                                kvm[s, h, :, 0:NWIN, :], 1.0, 0.0,
                                                ALU.mult, ALU.add).then_inc(placed["pool"], 1)
                if i % 2 == 1 and i + 1 < TILES:
                    r = (i + 1) // 2
                    n = grow(R0, i, r)
                    if i >= 1:
                        pool.wait_ge(placed["pool"], N_POOL * (T + 1))
                    pool.wait_ge(qraw_ready, n + 1)
                    col = qraw[:].rearrange("p (a c) -> p a c", c=WS)
                    hcol = qh[:].rearrange("p (a c) -> p a c", c=WS)
                    nc.gpsimd.tensor_tensor(qm[:], col[:, :, 1], col[:, :, 2], ALU.add).then_inc(q_step, 1)
                    pool.wait_ge(q_step, 6 * n + 1)
                    nc.gpsimd.tensor_tensor(hcol[:, :, 3], qm[:], col[:, :, 3], ALU.add)
                    nc.gpsimd.tensor_tensor(hcol[:, :, 0], qm[:], col[:, :, 0], ALU.add).then_inc(q_step, 1)
                    pool.wait_ge(q_step, 6 * n + 2)
                    nc.gpsimd.tensor_tensor(hcol[:, :, 1:3], hcol[:, :, 0:1].to_broadcast([P, MT * ROW_TOK // 4, 2]),
                                            col[:, :, 3:4].to_broadcast([P, MT * ROW_TOK // 4, 2]),
                                            ALU.add).then_inc(q_step, 1)
                    pool.wait_ge(q_step, 6 * n + 3)
                    row = qh[:].rearrange("p (a r c) -> p a r c", r=WS, c=WS)
                    srow = qsum[:].rearrange("p (a r c) -> p a r c", r=WS, c=WS)
                    mid = qm[:].rearrange("p (a c) -> p a c", c=WS)
                    nc.gpsimd.tensor_tensor(mid, row[:, :, 1, :], row[:, :, 2, :], ALU.add).then_inc(q_step, 1)
                    pool.wait_ge(q_step, 6 * n + 4)
                    if i >= 1:
                        pool.wait_ge(qp_ready, n)
                    nc.gpsimd.tensor_tensor(srow[:, :, 3, :], mid, row[:, :, 3, :], ALU.add).then_inc(q_step, 1)
                    nc.gpsimd.tensor_tensor(srow[:, :, 0, :], mid, row[:, :, 0, :], ALU.add).then_inc(q_step, 1)
                    pool.wait_ge(q_step, 6 * n + 6)
                    nc.gpsimd.tensor_tensor(srow[:, :, 1:3, :],
                                            srow[:, :, 0:1, :].to_broadcast([P, MT * WIN_PER_ROW, 2, WS]),
                                            row[:, :, 3:4, :].to_broadcast([P, MT * WIN_PER_ROW, 2, WS]),
                                            ALU.add).then_inc(qsum_ready, 1)
                if i % 2 == 0 and 0 <= (i - 4) // 2 < ROWS - 2:
                    r = (i - 4) // 2
                    pool.wait_ge(placed["pool"], N_POOL * (T + 1 if i < TILES else T))
                    add_row(b, grow(R0, i, r), lrow(c, i, r))

            def add_row(b, n, row):
                pool.wait_ge(y_ready, n + 1)
                for mt in range(MT):
                    xrow = xs_row(b % 2, mt, row).rearrange("p o (r w c) -> p (o w) r c", r=WS, c=WS)
                    last = nc.gpsimd.tensor_tensor(
                        xrow, yb[:, mt, :].rearrange("p (w r c) -> p w r c", r=WS, c=WS), xrow, ALU.add)
                last.then_inc(out_ready, 1)

            with pool.Fori(0, B) as b:
                slots(pool, b, slot, False)
                pool.wait_ge(placed["pool"], (b + 1) * (N_POOL * TILES))
                for row in (ROWS - 2, ROWS - 1):
                    add_row(b, b * ROWS + row, row)


def kernel(x, L0_conv_weight, L1_conv_qkv_w, L1_conv_proj_w, L1_conv_bn_gamma, L1_conv_bn_beta,
           L1_conv_bn_mean, L1_conv_bn_var):
    import concourse.bacc as bacc
    from concourse.bass_utils import run_bass_kernel_spmd

    def channels_first(w, split):
        return np.ascontiguousarray(w.reshape((split, P) + w.shape[1:]).swapaxes(0, 1))

    conv = channels_first(np.asarray(L0_conv_weight).reshape(C, C, TAPS * TAPS).transpose(1, 2, 0), KT)
    heads = np.asarray(L1_conv_qkv_w).reshape(C // DIM, 3, DIM, C).transpose(3, 1, 0, 2).reshape(C, 3 * C)
    qkv = channels_first(heads, KT)
    proj = channels_first(np.asarray(L1_conv_proj_w).T, G)
    bn = np.stack([np.asarray(v).reshape(MT, P).T for v in
                   (L1_conv_bn_gamma, L1_conv_bn_beta, L1_conv_bn_mean, L1_conv_bn_var)], axis=1)

    chan = np.arange(P)
    gavg = (chan[:, None] // GN_GROUP == chan[None, :] // GN_GROUP).astype(np.float32) / GN_GROUP
    tok = np.arange(TT)
    y, xx = tok % TOK // WS, tok % WS
    pool_m = ((tok[:, None] // TOK == tok[None, :] // TOK) & (abs(y[:, None] - y[None, :]) <= 2)
              & (abs(xx[:, None] - xx[None, :]) <= 2)).astype(np.float32)
    hmask = (chan[:, None] % 32 // DIM == np.arange(HEADS_Q)[None, :]).astype(np.float32)
    vinit = np.zeros((TT, SLOTS, 2 * C // 32, 32), np.float32)
    vinit[tok, NWIN, :, tok // TOK] = 1.0

    arrays = {
        "x": np.asarray(x).reshape(B, C, HW), "w_conv": conv,
        "w_q": np.ascontiguousarray(qkv[:, :, 0:C]), "w_kv": np.ascontiguousarray(qkv[:, :, C:]),
        "w_proj": proj, "bn": np.ascontiguousarray(bn), "gavg": gavg, "pool_m": pool_m,
        "ident": np.eye(P, dtype=np.float32), "hmask": hmask, "vinit": vinit.reshape(TT, SLOTS, 2, C),
    }
    nc = bacc.Bacc("TRN2", target_bir_lowering=False, num_devices=1)
    args = [nc.dram_tensor(n, a.shape, F32, kind="ExternalInput").ap() for n, a in arrays.items()]
    out = nc.dram_tensor("out", (B, C, H, W), F32, kind="ExternalOutput").ap()
    build(nc, *args, out.rearrange("b c h w -> b c (h w)"))
    r = run_bass_kernel_spmd(nc, [arrays], core_ids=[0])
    return r.results[0]["out"]
```

```python
import numpy as np

import concourse.bass as bass
from concourse import mybir
from contextlib import ExitStack

F32 = mybir.dt.float32
F32R = mybir.dt.float32r
ALU = mybir.AluOpType
ACT = mybir.ActivationFunctionType

B, C, H, W = 8, 256, 56, 56
P = 128
KT = C // P
MT = C // P
HW = H * W
TAPS = 3
PADW = W + 2
PRODUCTS = (1, 2, 0, 3)
PARTS = ((0, 0), (0, 1), (1, 0))
PAIRS = W // 2
CONV_H = 14
CONV_CHUNKS = H // CONV_H
CONV_IN = CONV_H + 2
CONV_N = CONV_H * PAIRS
CONV_D = KT * CONV_IN * PAIRS
CONV_STEPS = CONV_CHUNKS * len(PRODUCTS)
XP_STEPS = 2 * CONV_CHUNKS - 1
TAPS_K = KT * TAPS * C
WS = 4
TOK = WS * WS
WIN_PER_ROW = W // WS
ROWS = H // WS
ROW_TOK = WIN_PER_ROW * TOK
NWIN = WIN_PER_ROW // 2
TT = NWIN * TOK
TILES = 2 * ROWS
CHUNKS = TILES // 4
CHUNK = HW // CHUNKS
DIM = 8
G = 2 * C // P
HEADS_G = P // DIM
QUADS = P // 32
HEADS_Q = 32 // DIM
KVW = QUADS * HEADS_Q * (DIM + 1)
QW = HEADS_Q * (DIM + 1)
SLOTS = NWIN + 1
GN_GROUP = C // 32
GN_EPS = 1e-5
BN_EPS = 1e-5
DEN_EPS = 1e-15
POOL_SCALE = 1.0 / 25.0
BATCHES = ((0, 3), (3, 2), (5, 2))
T_A = 4
HEAD = (ROWS - 2) * ROW_TOK
DMA = 16

WARM_GROUP_NORM, WARM_FIRST_ROW, WARM_SPLIT, WARM_FIRST_TILE = 4, 16, 6, 13
WARM_LAST_TILE, WARM_START = 9, 22

CONSTS = 7

BANK_Q = 0
BANK_TA = 1
BANK_KV = 2
BANK_S = (3, 4)
BANK_G = 3
BANK_O = (5, 6, 7)
BANK_TB = 7
BANK_IDLE = 6
BANK_C = ((5, 6), (3, 4))

PLACE = {"act": ((0, 0), (0, 1), (1, 0)), "pool": ((0, 2), (0, 3), (1, 1)), "dve": ((1, 2), (1, 3))}


def build(nc, x, w_conv, w_q, w_kv, w_proj, bn, gavg, pool_m, ident, hmask, vinit, out):
    ctx = ExitStack()
    with ctx:
        def sb(name, shape, dtype=F32):
            return ctx.enter_context(nc.sbuf_tensor(name, shape, dtype))

        def sem(name):
            return ctx.enter_context(nc.semaphore(name))

        wc = sb("wc", [P, 2, 4, KT * TAPS, C], F32R)
        wq = sb("wq", [P, KT, C])
        wkv = sb("wkv", [P, 2, KT, 2 * C], F32R)
        wp = sb("wp", [P, G, C])
        bnp = sb("bnp", [P, 4, MT])
        gav = sb("gav", [P, P])
        poolm = sb("poolm", [TT, TT], F32R)
        idn = sb("idn", [P, P])
        hm = sb("hm", [P, HEADS_Q])
        xs = sb("xs", [P, 2, KT, HW])
        xp = sb("xp", [P, KT, CONV_IN, PADW])
        dp = sb("dp", [P, 2, 2, CONV_D], F32R)
        st0 = sb("st0", [P, KT, CHUNKS, 6])
        st1 = sb("st1", [P, KT, 2 * CONV_CHUNKS, 6])
        mv = sb("mv", [P, KT, 2])
        dev = sb("dev", [P, 8, KT])
        gn0 = sb("gn0", [P, 2, KT])
        gn1 = sb("gn1", [P, 2, KT])
        bni = sb("bni", [P, MT])
        bns = sb("bns", [P, MT])
        bnt = sb("bnt", [P, 6, MT])
        xh = sb("xh", [P, 2, KT, ROW_TOK])
        qs = sb("qs", [P, G, 2, ROW_TOK + TOK])
        raw = sb("raw", [TT, 2, 3 * C])
        kr = sb("kr", [TT, 2, 2 * C])
        ve = sb("ve", [TT, SLOTS, 2, C])
        kvm = sb("kvm", [P, 2, 2, SLOTS, QW])
        kvb = sb("kvb", [P, G, NWIN, KVW])
        den = sb("den", [P, NWIN, HEADS_G])
        rcp = sb("rcp", [P, NWIN, HEADS_G])
        ao = sb("ao", [P, NWIN, P])
        at = sb("at", [P, G, 2, ROW_TOK])
        yb = sb("yb", [P, MT, ROW_TOK])

        ps = ctx.enter_context(nc.psum_tensor("ps", [P, 8, 512], F32))

        xp_flat = xp[:].rearrange("p k y x -> p (k y x)")
        QN = MT * ROW_TOK
        qraw, qh, qsum = (xp_flat[:, n * QN:(n + 1) * QN] for n in range(3))
        qm = xp_flat[:, 3 * QN:3 * QN + QN // 4]
        dp_flat = dp[:].rearrange("p a b n -> p (a b n)")
        kv_part = tuple(dp_flat[0:TT, n * 2 * C:(n + 1) * 2 * C] for n in range(2))
        XN = KT * ROW_TOK
        xh_part = tuple(tuple(dp_flat[:, 4 * C + (2 * rp + n) * XN:4 * C + (2 * rp + n + 1) * XN]
                              .rearrange("p (k n) -> p k n", k=KT) for n in range(2)) for rp in range(2))
        at_flat = at[:].rearrange("p g r n -> p (g r n)")
        wkv_raw = at_flat[:, 0:KT * 2 * C].rearrange("p (k o) -> p k o", k=KT)
        poolm_raw = at_flat[0:TT, KT * 2 * C:KT * 2 * C + TT]

        dt = (xh[:].rearrange("p a k n -> p (a k n)"), ao[:].rearrange("p w n -> p (w n)"))
        wspace = xs[:, 1].rearrange("p k n -> p (k n)")
        wraw = wspace[:, 0:TAPS * TAPS_K].rearrange("p (a x o) -> p a x o", x=TAPS, o=C)
        wsum = wspace[:, TAPS * TAPS_K:(TAPS + 1) * TAPS_K].rearrange("p (a o) -> p a o", o=C)
        wouter = xp_flat[:, 0:TAPS_K].rearrange("p (a o) -> p a o", o=C)
        wprod = (wraw[:, :, 0, :], wsum, wraw[:, :, 1, :], wraw[:, :, 2, :])

        x_loaded = sem("x_loaded")
        x_tail_loaded = sem("x_tail_loaded")
        w_loaded = sem("w_loaded")
        gav_loaded = sem("gav_loaded")
        bn_loaded = sem("bn_loaded")
        c_loaded = sem("c_loaded")
        ve_loaded = sem("ve_loaded")
        stored = sem("stored")
        conv_done = sem("conv_done")
        gsum_done = sem("gsum_done")
        kv_done = sem("kv_done")
        pool_done = sem("pool_done")
        q_done = sem("q_done")
        ktv_done = sem("ktv_done")
        att_done = sem("att_done")
        tr_done = sem("tr_done")
        proj_done = sem("proj_done")
        raw_ready = sem("raw_ready")
        kp_ready = sem("kp_ready")
        vp_ready = sem("vp_ready")
        placed = {e: sem("placed_" + e) for e in PLACE}
        q_ready = sem("q_ready")
        qraw_ready = sem("qraw_ready")
        at_ready = sem("at_ready")
        y_ready = sem("y_ready")
        w_high = sem("w_high")
        att_w_high = sem("att_w_high")
        xh_high = sem("xh_high")
        kv_high = sem("kv_high")
        d_high = sem("d_high")
        root_ready = sem("root_ready")
        set_up = sem("set_up")
        conv_added = sem("conv_added")
        w_step = sem("w_step")
        w_ready = sem("w_ready")
        xp_ready = sem("xp_ready")
        d_ready = sem("d_ready")
        d_low = sem("d_low")
        gn_in = sem("gn_in")
        gn_step = sem("gn_step")
        gn_var = sem("gn_var")
        st0_done = sem("st0_done")
        st1_done = sem("st1_done")
        bn_ready = sem("bn_ready")
        bn_step = sem("bn_step")
        xh_ready = sem("xh_ready")
        xh_low = sem("xh_low")
        kv_low = sem("kv_low")
        att_w_low = sem("att_w_low")
        k_ready = sem("k_ready")
        masked = sem("masked")
        den_ready = sem("den_ready")
        rcp_ready = sem("rcp_ready")
        ao_ready = sem("ao_ready")
        qp_ready = sem("qp_ready")
        q_step = sem("q_step")
        qsum_ready = sem("qsum_ready")
        out_ready = sem("out_ready")

        block = ctx.enter_context(nc.Block())

        N_ACT, N_POOL, N_DVE = (len(PLACE[e]) for e in ("act", "pool", "dve"))

        def first_slots(b, slot, last):
            slot(b * TILES - 1, b * ROWS, -1, b, 0, last)
            for t in range(4):
                slot(b * TILES + t, b * ROWS, t, b, 0, last)

        def later_slots(eng, b, slot, last):
            with eng.Fori(1, CHUNKS - 1) as c:
                for t in range(4):
                    slot(b * TILES + c * 4 + t, b * ROWS + c * 2, 4 + t, b, c, last)
            for i in range(TILES - 4, TILES + 1):
                slot(b * TILES + i, b * ROWS + (i // 4) * 2, i, b, i // 4, last)

        def slots(eng, b, slot, last):
            first_slots(b, slot, last)
            later_slots(eng, b, slot, last)

        def grow(R0, i, r):
            return R0 + (r - (2 * (i // 4) if i >= 0 else 0))

        def lrow(c, i, r):
            return c * 2 + (r - (2 * (i // 4) if i >= 0 else 0))

        def xs_row(par, mt, row, n=ROW_TOK):
            return xs[:, bass.ds(par, 1), mt, bass.ds(row * ROW_TOK, n)]

        def alone(eng, value):
            value = value if isinstance(value, int) else eng.to_reg(value)
            eng.wait_ge(w_loaded, DMA)
            return value

        @block.sync
        def _(sp):
            def load_x(img, part):
                lo, hi, loaded = ((0, HEAD, x_loaded), (HEAD, HW, x_tail_loaded))[part]
                for kt in range(KT):
                    sp.dma_start(xs[:, bass.ds(img % 2, 1), kt, lo:hi],
                                 x[bass.ds(img, 1), kt * P:(kt + 1) * P, lo:hi].rearrange("o p n -> p o n")).then_inc(loaded, DMA)

            def store_row(b, n, row):
                sp.wait_ge(out_ready, alone(sp, n + 1))
                for mt in range(MT):
                    sp.dma_start(out[bass.ds(b, 1), mt * P:(mt + 1) * P, bass.ds(row * ROW_TOK, ROW_TOK)]
                                 .rearrange("o p n -> p o n"),
                                 xs_row(b % 2, mt, row)).then_inc(stored, DMA)

            sp.dma_start(bnp[:], bn).then_inc(bn_loaded, DMA)
            sp.dma_start(wspace[:, 0:TAPS * TAPS_K], w_conv).then_inc(w_loaded, DMA)
            sp.dma_start(gav[:], gavg).then_inc(gav_loaded, DMA)
            load_x(0, 0)
            load_x(0, 1)
            for dst, src in ((wq[:], w_q), (wkv_raw, w_kv), (wp[:], w_proj), (poolm_raw, pool_m), (idn[:], ident), (hm[:], hmask)):
                sp.dma_start(dst, src).then_inc(c_loaded, DMA)
            sp.dma_start(ve[:], vinit).then_inc(c_loaded, DMA)
            sp.wait_ge(c_loaded, CONSTS * DMA)
            sp.wait_ge(x_loaded, KT * DMA)
            sp.wait_ge(x_tail_loaded, KT * DMA)
            sp.wait_ge(w_ready, len(PRODUCTS))
            load_x(1, 0)
            load_x(1, 1)

            def slot(T, R0, i, b, c, last):
                if i + 1 < TILES:
                    par = (i + 1) % 2
                    sp.wait_ge(vp_ready, alone(sp, T + 2))
                    if i >= 0:
                        sp.wait_ge(ktv_done, alone(sp, 2 * T + 2))
                    for w in range(NWIN):
                        sp.dma_start(ve[w * TOK:(w + 1) * TOK, w].rearrange("p h c -> p (h c)"),
                                     raw[w * TOK:(w + 1) * TOK, par, C:3 * C]).then_inc(ve_loaded, DMA)
                if i % 2 == 0 and 0 <= (i - 4) // 2 < ROWS - 2:
                    r = (i - 4) // 2
                    store_row(b, grow(R0, i, r), lrow(c, i, r))

            def last_rows(b):
                for row in (ROWS - 2, ROWS - 1):
                    store_row(b, b * ROWS + row, row)

            first_slots(0, slot, False)
            with sp.Fori(0, B - 2) as b:
                later_slots(sp, b, slot, False)
                sp.wait_ge(stored, alone(sp, (b * ROWS + ROWS - 2) * (MT * DMA)))
                load_x(b + 2, 0)
                last_rows(b)
                first_slots(b + 1, slot, False)
                sp.wait_ge(stored, alone(sp, (b + 1) * (MT * ROWS * DMA)))
                load_x(b + 2, 1)
            later_slots(sp, B - 2, slot, False)
            last_rows(B - 2)
            slots(sp, B - 1, slot, True)
            last_rows(B - 1)
            sp.wait_ge(stored, B * MT * ROWS * DMA)

        @block.tensor
        def _(pe):
            def keep_warm(n, bank=BANK_IDLE):
                for _ in range(n):
                    nc.tensor.matmul(ps[:, bank, :], wkv[:, 0, 0, 0:P], wkv[:, 0, 0, :], start=True, stop=True)

            def conv(img, first=False):
                with pe.Fori(0, CONV_CHUNKS) as c:
                    for kk, k in enumerate(PRODUCTS):
                        v = (img * CONV_CHUNKS + c) * len(PRODUCTS) + kk
                        if first:
                            pe.wait_ge(w_ready, kk + 1)
                        pe.wait_ge(d_low, v + 1)
                        for mt in range(MT):
                            pe.wait_ge(conv_added, 2 * v + mt + 1)
                            n = 0
                            for part_w, part_d in PARTS:
                                for kt in range(KT):
                                    for dy in range(TAPS):
                                        d0 = (kt * CONV_IN + dy) * PAIRS
                                        last = nc.tensor.matmul(
                                            ps[:, BANK_C[kk % 2][mt], 0:CONV_N],
                                            wc[:, part_w, k, kt * TAPS + dy, mt * P:(mt + 1) * P],
                                            dp[:, kk % 2, part_d, d0:d0 + CONV_N],
                                            start=(n == 0), stop=(n == len(PARTS) * KT * TAPS - 1))
                                        n += 1
                            last.then_inc(conv_done, 1)

            def group_sums(n, steps=(0, 1)):
                for s in steps:
                    if s == 1 and len(steps) == 2:
                        keep_warm(WARM_GROUP_NORM)
                    pe.wait_ge(gn_in, 2 * n + s + 1)
                    src = mv[:, :, 0] if s == 0 else dev[:, 1, :]
                    nc.tensor.matmul(ps[:, BANK_G, s * KT:(s + 1) * KT], gav[:], src,
                                     start=True, stop=True).then_inc(gsum_done, 1)

            def q_of_row(R0, i):
                r = (i + 1) // 2
                if i >= 5:
                    pe.wait_ge(y_ready, grow(R0, i, (i - 5) // 2) + 1)
                for mt in range(MT):
                    for kt in range(KT):
                        last = nc.tensor.matmul(ps[:, BANK_Q, mt * ROW_TOK:(mt + 1) * ROW_TOK],
                                                wq[:, kt, mt * P:(mt + 1) * P], xh[:, r % 2, kt, :],
                                                start=(kt == 0), stop=(kt == KT - 1))
                last.then_inc(q_done, 1)

            def slot(T, R0, i, b, c, last_image):
                par1, par = (i + 1) % 2, i % 2
                if i + 1 < TILES:
                    rp = ((i + 1) // 2) % 2
                    if i % 2 == 1:
                        pe.wait_ge(xh_low, grow(R0, i, (i + 1) // 2) + 1)
                    if i >= 0:
                        pe.wait_ge(raw_ready, T + 1)
                    off = ((i + 1) % 2) * TT
                    for n, (part_w, part_x) in enumerate(PARTS):
                        for kt in range(KT):
                            last = nc.tensor.matmul(
                                ps[0:TT, BANK_KV, :], xh_part[rp][part_x][:, kt, off:off + TT],
                                wkv[:, part_w, kt, :], start=(n == 0 and kt == 0),
                                stop=(n == len(PARTS) - 1 and kt == KT - 1))
                    last.then_inc(kv_done, 1)
                if not last_image and i in (TILES - 4, TILES - 3):
                    pe.wait_ge(masked, 2 * T)
                    group_sums(2 * b + 2, (i - (TILES - 4),))
                if i == TILES and not last_image:
                    keep_warm(WARM_LAST_TILE, BANK_KV)
                if 1 <= i <= TILES:
                    j = i - 1
                    rp, off = (j // 2) % 2, (j % 2) * TT
                    pe.wait_ge(placed["act"], N_ACT * T)
                    pe.wait_ge(placed["pool"], N_POOL * T)
                    pe.wait_ge(placed["dve"], N_DVE * T)
                    pe.wait_ge(q_ready, grow(R0, i, j // 2) + 1)
                    pe.wait_ge(qp_ready, grow(R0, i, j // 2) + 1)
                    for n, (w0, nw) in enumerate(BATCHES):
                        if j >= 1:
                            pe.wait_ge(ao_ready, 3 * T + (n - 5))
                            if BANK_O[n] == BANK_TB:
                                pe.wait_ge(at_ready, 2 * T - 2)
                        for w in range(w0, w0 + nw):
                            for g in range(G):
                                o = off + w * TOK
                                last = nc.tensor.matmul(
                                    ps[32 * g:32 * g + 32, BANK_O[n], (w - w0) * KVW:(w - w0 + 1) * KVW],
                                    qs[:, g, rp, o:o + 2 * TOK], kvb[:, g, w, :], start=True, stop=True)
                        last.then_inc(att_done, 1)
                if i == -1:
                    q_of_row(R0, i)
                if i + 1 < TILES:
                    if i == 0:
                        keep_warm(WARM_SPLIT)
                    pe.wait_ge(kv_low, T + 2)
                    if i >= 2:
                        pe.wait_ge(at_ready, 2 * T - 3)
                    nc.tensor.matmul(ps[0:TT, BANK_TA, :], poolm[:], kv_part[0], start=True, stop=False)
                    nc.tensor.matmul(ps[0:TT, BANK_TA, :], poolm[:], kv_part[1],
                                     start=False, stop=True).then_inc(pool_done, 1)
                if 0 <= i < TILES:
                    if i == 0:
                        keep_warm(WARM_FIRST_TILE)
                    for h in range(2):
                        if h == 0 and not last_image and i == TILES - 4:
                            pe.wait_ge(gn_step, 8 * (2 * b + 2) + 1)
                        if h == 0 and not last_image and i == TILES - 3:
                            pe.wait_ge(gn_var, 2 * b + 3)
                        pe.wait_ge(ve_loaded, (T + 1) * (NWIN * DMA))
                        pe.wait_ge(k_ready if h == 0 else kp_ready, T + 1)
                        if i >= 1:
                            pe.wait_ge(masked, 2 * T + (h - 1))
                        for gg in range(2):
                            for q in range(QUADS):
                                k0 = h * C + gg * P + 32 * q
                                v0 = gg * P + 32 * q
                                last = nc.tensor.matmul(
                                    ps[32 * q:32 * q + 32, BANK_S[h], gg * C:(gg + 1) * C],
                                    kr[:, par, k0:k0 + 32], ve[:, :, h, v0:v0 + 32], start=True, stop=True)
                        last.then_inc(ktv_done, 1)
                if i % 2 == 1 and i >= 1 and i + 1 < TILES:
                    q_of_row(R0, i)
                if i % 2 == 0 and 0 <= (i - 4) // 2 < ROWS - 2:
                    r = (i - 4) // 2
                    pe.wait_ge(at_ready, 2 * T - 4)
                    if i < TILES:
                        pe.wait_ge(q_ready, grow(R0, i, i // 2) + 1)
                        pe.wait_ge(qraw_ready, grow(R0, i, i // 2) + 1)
                    project(r % 2)
                if 1 <= i <= TILES:
                    for n, (w0, w1) in enumerate(((0, T_A), (T_A, NWIN))):
                        pe.wait_ge(ao_ready, 3 * T + (n - 1))
                        if n == 0 and i < TILES - 1:
                            pe.wait_ge(vp_ready, T + 2)
                        for w in range(w0, w1):
                            last = nc.tensor.transpose(ps[:, BANK_TA if n == 0 else BANK_TB, (w - w0) * P:(w - w0 + 1) * P],
                                                       ao[:, w, :], idn[:])
                        last.then_inc(tr_done, 1)

            def project(rp):
                for mt in range(MT):
                    for g in range(G):
                        last = nc.tensor.matmul(ps[:, BANK_Q, mt * ROW_TOK:(mt + 1) * ROW_TOK],
                                                wp[:, g, mt * P:(mt + 1) * P], at[:, g, rp, :],
                                                start=(g == 0), stop=(g == G - 1))
                last.then_inc(proj_done, 1)

            def last_row(b, row):
                pe.wait_ge(at_ready, (b + 1) * (2 * TILES))
                pe.wait_ge(y_ready, b * ROWS + row)
                project(row % 2)

            pe.wait_ge(gav_loaded, DMA)
            group_sums(0, (0,))
            group_sums(0, (1,))
            for _ in range(WARM_START):
                nc.tensor.matmul(ps[:, BANK_IDLE, 0:P], gav[:], gav[:], start=True, stop=True)
            conv(0, first=True)
            group_sums(1)
            pe.wait_ge(att_w_low, 1)
            pe.wait_ge(c_loaded, CONSTS * DMA)
            with pe.Fori(0, B - 1) as b:
                slots(pe, b, slot, False)
                conv(b + 1)
                last_row(b, ROWS - 2)
                group_sums(2 * b + 3)
                last_row(b, ROWS - 1)
                keep_warm(WARM_FIRST_ROW)
                pe.wait_ge(y_ready, (b + 1) * ROWS)
            slots(pe, B - 1, slot, True)
            last_row(B - 1, ROWS - 2)
            last_row(B - 1, ROWS - 1)

        @block.scalar
        def _(act):
            def root(n):
                act.wait_ge(gn_var, n + 1)
                nc.scalar.activation(dev[:, 3, :], dev[:, 2, :], ACT.Sqrt).then_inc(root_ready, 1)

            def split(v, kk, first=False):
                act.wait_ge(d_ready, v + 1)
                if not first:
                    act.wait_ge(conv_done, 2 * v - 2)
                nc.scalar.copy(dp[:, kk % 2, 0, :], dt[kk % 2]).then_inc(d_high, 1)

            def split_rest(img):
                with act.Fori(0, CONV_CHUNKS - 1) as c:
                    for kk in range(4):
                        split(img * CONV_STEPS + c * 4 + 2 + kk, kk)
                for kk in (2, 3):
                    split(img * CONV_STEPS + CONV_STEPS - 4 + kk, kk)

            def slot(T, R0, i, b, c, last_image):
                par1 = (i + 1) % 2
                if i == -1:
                    split_row(b * ROWS, 0)
                if i + 1 < TILES:
                    act.wait_ge(kv_done, T + 2)
                    if i >= 0:
                        act.wait_ge(pool_done, T + 1)
                    nc.scalar.copy(kv_part[0], ps[0:TT, BANK_KV, :]).then_inc(kv_high, 1)
                    act.wait_ge(kv_low, T + 2)
                    if i >= 1:
                        act.wait_ge(k_ready, T)
                        act.wait_ge(ve_loaded, T * (NWIN * DMA))
                    nc.scalar.copy(raw[:, par1, 0:2 * C], ps[0:TT, BANK_KV, :]).then_inc(raw_ready, 1)
                    act.wait_ge(pool_done, T + 2)
                    if i >= 1:
                        act.wait_ge(ktv_done, 2 * T)
                    nc.scalar.activation(kr[:, par1, C:2 * C], ps[0:TT, BANK_TA, 0:C], ACT.Relu,
                                         scale=POOL_SCALE).then_inc(kp_ready, 1)
                    nc.scalar.activation(raw[:, par1, 2 * C:3 * C], ps[0:TT, BANK_TA, C:2 * C], ACT.Copy,
                                         scale=POOL_SCALE).then_inc(vp_ready, 1)
                if i % 2 == 0 and (i + 2) // 2 < ROWS:
                    r = (i + 2) // 2
                    split_row(grow(R0, i, r), r % 2)
                if 0 <= i < TILES:
                    for h, q in PLACE["act"]:
                        act.wait_ge(masked, 2 * T + (h + 1))
                        if i >= 1:
                            act.wait_ge(att_done, 3 * T)
                        s = slice(32 * q, 32 * q + 32)
                        nc.scalar.copy(kvb[s, 2 * h:2 * h + 2, :, q * QW:(q + 1) * QW],
                                       kvm[s, h, :, 0:NWIN, :]).then_inc(placed["act"], 1)
                if i % 2 == 1 and i + 1 < TILES:
                    r = (i + 1) // 2
                    act.wait_ge(q_done, grow(R0, i, r) + 1)
                    if i >= 3:
                        act.wait_ge(att_done, 3 * T - 3)
                    nc.scalar.activation(qs[:, 0:MT, r % 2, 0:ROW_TOK],
                                         ps[:, BANK_Q, 0:MT * ROW_TOK].rearrange("p (m n) -> p m n", m=MT),
                                         ACT.Relu).then_inc(q_ready, 1)
                    if i >= 1:
                        act.wait_ge(qsum_ready, grow(R0, i, r))
                    nc.scalar.copy(qraw, ps[:, BANK_Q, 0:MT * ROW_TOK]).then_inc(qraw_ready, 1)
                if i == TILES and not last_image:
                    split((b + 1) * CONV_STEPS, 0)
                if 1 <= i <= TILES:
                    j = i - 1
                    rp, off = (j // 2) % 2, (j % 2) * TT
                    for n, (w0, w1) in enumerate(((0, T_A), (T_A, NWIN))):
                        act.wait_ge(tr_done, 2 * T + (n - 1))
                        src = ps[:, BANK_TA if n == 0 else BANK_TB, 0:(w1 - w0) * P]
                        nc.scalar.copy(
                            at[:, :, rp, off + w0 * TOK:off + w1 * TOK].rearrange("p g (w t) -> p w g t", t=TOK),
                            src.rearrange("p (w g t) -> p w g t", g=G, t=2 * TOK)[:, :, :, 0:TOK]).then_inc(at_ready, 1)
                if i % 2 == 0 and 0 <= (i - 4) // 2 < ROWS - 2:
                    r = (i - 4) // 2
                    batch_norm(grow(R0, i, r), first=(r == 0))
                if i == TILES - 3 and not last_image:
                    root(2 * b + 2)

            def split_row(n, rp):
                act.wait_ge(xh_ready, n + 1)
                nc.scalar.copy(xh_part[rp][0], xh[:, rp]).then_inc(xh_high, 1)

            def batch_norm(n, first=False):
                act.wait_ge(proj_done, n + 1)
                if not first:
                    act.wait_ge(out_ready, n)
                for mt in range(MT):
                    last = nc.scalar.activation(yb[:, mt, :], ps[:, BANK_Q, mt * ROW_TOK:(mt + 1) * ROW_TOK],
                                                ACT.Identity, bias=bns[:, mt:mt + 1], scale=bni[:, mt:mt + 1])
                last.then_inc(y_ready, 1)

            act.wait_ge(bn_step, 1)
            nc.scalar.activation(bnt[:, 1, :], bnt[:, 0, :], ACT.Sqrt).then_inc(bn_ready, 1)
            act.wait_ge(w_loaded, DMA)
            for n, k in enumerate((0, 3, 1, 2)):
                if n >= 2:
                    act.wait_ge(w_step, n + 2)
                nc.scalar.copy(wc[:, 0, k], wprod[k]).then_inc(w_high, 1)
            root(0)
            for kk in range(2):
                split(kk, kk, first=True)
            act.wait_ge(c_loaded, CONSTS * DMA)
            nc.scalar.copy(wkv[:, 0], wkv_raw).then_inc(att_w_high, 1)
            nc.scalar.copy(poolm[:], poolm_raw).then_inc(att_w_high, 1)
            split_rest(0)
            root(1)
            act.wait_ge(bn_step, 9)
            with act.Fori(0, B - 1) as b:
                slots(act, b, slot, False)
                split((b + 1) * CONV_STEPS + 1, 1)
                act.wait_ge(qsum_ready, (b + 1) * ROWS)
                split_rest(b + 1)
                batch_norm(b * ROWS + ROWS - 2)
                root(2 * b + 3)
                batch_norm(b * ROWS + ROWS - 1)
                act.wait_ge(out_ready, (b + 1) * ROWS)
            slots(act, B - 1, slot, True)
            batch_norm(B * ROWS - 2)
            batch_norm(B * ROWS - 1)

        @block.vector
        def _(dve):
            def flat(ap):
                return ap.rearrange("p o n -> p (o n)")

            def step(n, k, ins):
                ins.then_inc(gn_step, 1)
                dve.wait_ge(gn_step, 8 * n + k)

            def group_norm_start(n, stats, dst):
                channel_stats(n, stats)
                group_means(n, dst)
                group_variances(n)

            def channel_stats(n, stats):
                for kt in range(KT):
                    last = nc.vector.bn_aggr(mv[:, kt, :], stats[:, kt, :, :].rearrange("p c s -> p (c s)"))
                last.then_inc(gn_in, 1)

            def group_means(n, dst):
                dve.wait_ge(gn_in, 2 * n + 1)
                dve.wait_ge(gsum_done, 2 * n + 1)
                step(n, 1, nc.vector.tensor_copy(dst[:, 0, :], ps[:, BANK_G, 0:KT]))
                step(n, 2, nc.vector.tensor_tensor(dev[:, 0, :], mv[:, :, 0], dst[:, 0, :], ALU.subtract))
                step(n, 3, nc.vector.tensor_tensor(dev[:, 7, :], dev[:, 0, :], dev[:, 0, :], ALU.mult))
                nc.vector.tensor_tensor(dev[:, 1, :], dev[:, 7, :], mv[:, :, 1], ALU.add).then_inc(gn_in, 1)

            def group_variances(n):
                dve.wait_ge(gsum_done, 2 * n + 2)
                nc.vector.tensor_scalar(dev[:, 2, :], ps[:, BANK_G, KT:2 * KT], GN_EPS, None,
                                        ALU.add).then_inc(gn_var, 1)

            def group_norm_end(n, dst):
                dve.wait_ge(gn_var, n + 1)
                dve.wait_ge(root_ready, n + 1)
                step(n, 4, nc.vector.reciprocal(dev[:, 4, :], dev[:, 3, :]))
                step(n, 5, nc.vector.tensor_tensor(dev[:, 5, :], dev[:, 4, :], dev[:, 2, :], ALU.mult))
                step(n, 6, nc.vector.tensor_tensor(dev[:, 6, :], dev[:, 5, :], dev[:, 3, :], ALU.add))
                step(n, 7, nc.vector.tensor_scalar(dev[:, 7, :], dev[:, 6, :], 0.5, None, ALU.mult))
                step(n, 8, nc.vector.reciprocal(dst[:, 1, :], dev[:, 7, :]))

            def stats_x(par, c):
                for kt in range(KT):
                    last = nc.vector.bn_stats(st0[:, kt, bass.ds(c, 1), :].rearrange("p o s -> p (o s)"),
                                              flat(xs[:, bass.ds(par, 1), kt, bass.ds(c * CHUNK, CHUNK)]))
                return last

            def fill_xp(par, row, rows, to):
                for kt in range(KT):
                    last = nc.vector.tensor_scalar(
                        xp[:, kt, to:to + rows, 1:W + 1],
                        xs[:, bass.ds(par, 1), kt, bass.ds(row * W, rows * W)].rearrange("p o (y x) -> p (o y) x", x=W),
                        gn0[:, 0, kt:kt + 1], gn0[:, 1, kt:kt + 1], ALU.subtract, ALU.mult)
                return last

            def first_chunk(img, par):
                for col in (0, PADW - 1):
                    nc.vector.memset(xp[:, :, 1:CONV_IN, col], 0.0)
                nc.vector.memset(xp[:, :, 0, :], 0.0)
                fill_xp(par, 0, CONV_IN - 1, 1).then_inc(xp_ready, 1)

            def next_chunk(img, par, c, edge):
                dve.wait_ge(d_ready, alone(dve, img * CONV_STEPS + c * 4 + 4))
                nc.vector.tensor_copy(xp[:, :, 0:2, :], xp[:, :, CONV_H:CONV_IN, :]).then_inc(xp_ready, 1)
                dve.wait_ge(xp_ready, alone(dve, img * XP_STEPS + c * 2 + 2))
                if edge:
                    nc.vector.memset(xp[:, :, CONV_IN - 1, :], 0.0)
                fill_xp(par, c * CONV_H + CONV_IN - 1, CONV_H - edge, 2).then_inc(xp_ready, 1)

            def product_inputs(img, c, kk, first=False):
                if kk == 0:
                    dve.wait_ge(xp_ready, alone(dve, img * XP_STEPS + c * 2 + 1))
                if not first:
                    dve.wait_ge(d_low, alone(dve, (img * CONV_CHUNKS + c) * 4 + kk - 1))
                d = [xp[:, :, :, j:j + W - 1:2].rearrange("p k y x -> p (k y) x") for j in range(4)]
                in0, in1, op = ((d[0], d[2], ALU.subtract), (d[1], d[2], ALU.add),
                                (d[2], d[1], ALU.subtract), (d[1], d[3], ALU.subtract))[PRODUCTS[kk]]
                nc.vector.tensor_tensor(dt[kk % 2].rearrange("p (y x) -> p y x", x=PAIRS),
                                        in0, in1, op).then_inc(d_ready, 1)

            def low_parts(v, kk):
                dve.wait_ge(d_high, v + 1)
                nc.vector.tensor_tensor(dp[:, kk % 2, 1, :], dt[kk % 2], dp[:, kk % 2, 0, :].bitcast(F32),
                                        ALU.subtract).then_inc(d_low, 1)

            def conv(img):
                par = img % 2

                def chunk(c, left):
                    for kk, k in enumerate(PRODUCTS):
                        v = (img * CONV_CHUNKS + c) * 4 + kk
                        if left or kk < 3:
                            low_parts(v + 1, (kk + 1) % 4)
                        if left and kk == 2:
                            next_chunk(img, par, c, left == 1)
                        if left or kk < 2:
                            product_inputs(img, c + (kk + 2) // 4, (kk + 2) % 4)
                        for mt in range(MT):
                            dve.wait_ge(conv_done, 2 * v + mt + 1)
                            if k != PRODUCTS[0]:
                                dve.wait_ge(conv_added, 2 * v + mt + 3)
                            pair = flat(xs[:, bass.ds(par, 1), mt, bass.ds(c * (CONV_H * W), CONV_H * W)]) \
                                .rearrange("p (n e) -> p n e", e=2)
                            for e, op in {0: ((0, ALU.add),), 1: ((0, ALU.add), (1, ALU.add)),
                                          2: ((0, ALU.add), (1, ALU.subtract)), 3: ((1, ALU.subtract),)}[k]:
                                last = nc.vector.tensor_tensor(pair[:, :, e], pair[:, :, e],
                                                               ps[:, BANK_C[kk % 2][mt], 0:CONV_N], op)
                            last.then_inc(conv_added, 1)
                            if k == PRODUCTS[-1]:
                                dve.wait_ge(conv_added, alone(dve, 2 * v + mt + 5))
                                for half in range(2):
                                    last = nc.vector.bn_stats(
                                        st1[:, mt, bass.ds(2 * c + half, 1), :].rearrange("p o s -> p (o s)"),
                                        flat(xs[:, bass.ds(par, 1), mt,
                                                bass.ds(c * (CONV_H * W) + half * CONV_N, CONV_N)]))
                                last.then_inc(st1_done, 1)

                with dve.Fori(0, CONV_CHUNKS - 2) as c:
                    chunk(c, 2)
                chunk(CONV_CHUNKS - 2, 1)
                chunk(CONV_CHUNKS - 1, 0)
                dve.wait_ge(st1_done, alone(dve, (img + 1) * (CONV_CHUNKS * MT)))

            def normalize_row(b, row, rp):
                for kt in range(KT):
                    src = xs[:, bass.ds(b % 2, 1), kt, bass.ds(row * ROW_TOK, ROW_TOK)]
                    last = nc.vector.tensor_scalar(
                        xh[:, rp, kt, :].rearrange("p (w r c) -> p w r c", r=WS, c=WS),
                        src.rearrange("p o (r w c) -> p (o w) r c", r=WS, c=WS),
                        gn1[:, 0, kt:kt + 1], gn1[:, 1, kt:kt + 1], ALU.subtract, ALU.mult)
                last.then_inc(xh_ready, 1)

            def row_low(n, rp):
                dve.wait_ge(xh_high, n + 1)
                nc.vector.tensor_tensor(xh_part[rp][1], xh[:, rp], xh_part[rp][0].bitcast(F32),
                                        ALU.subtract).then_inc(xh_low, 1)

            def slot(T, R0, i, b, c, last_image):
                par1 = (i + 1) % 2
                if i == -1:
                    normalize_row(b, 0, 0)
                    row_low(b * ROWS, 0)
                if not last_image:
                    if (i % 4 == 1 and i < TILES - 4) or i == TILES - 4:
                        if i == 1:
                            dve.wait_ge(x_loaded, (b + 2) * (KT * DMA))
                        if i == TILES - 4:
                            dve.wait_ge(x_tail_loaded, (b + 2) * (KT * DMA))
                        stats_x((b + 1) % 2, c).then_inc(st0_done, 1)
                    if i == TILES - 4:
                        dve.wait_ge(st0_done, alone(dve, (b + 2) * CHUNKS))
                        channel_stats(2 * b + 2, st0)
                if i + 1 < TILES:
                    dve.wait_ge(kv_high, T + 2)
                    nc.vector.tensor_tensor(kv_part[1], ps[0:TT, BANK_KV, :], kv_part[0].bitcast(F32),
                                            ALU.subtract).then_inc(kv_low, 1)
                if i == TILES - 4 and not last_image:
                    group_means(2 * b + 2, gn0)
                if i == TILES - 3 and not last_image:
                    group_variances(2 * b + 2)
                if i % 2 == 0 and (i + 2) // 2 < ROWS:
                    r = (i + 2) // 2
                    if i >= 2:
                        dve.wait_ge(kv_done, T)
                        dve.wait_ge(q_done, grow(R0, i, r) - 1)
                    normalize_row(b, lrow(c, i, r), r % 2)
                if 1 <= i <= TILES:
                    for n, (w0, nw) in enumerate(BATCHES):
                        dve.wait_ge(att_done, 3 * T + (n - 2))
                        o = ps[:, BANK_O[n], 0:nw * KVW].rearrange("p (w h m) -> p w h m", w=nw, m=DIM + 1)
                        nc.vector.tensor_scalar(den[:, w0:w0 + nw, :], o[:, :, :, DIM], DEN_EPS, None,
                                                ALU.add).then_inc(den_ready, 1)
                        dve.wait_ge(den_ready, 3 * T + (n - 2))
                        nc.vector.reciprocal(rcp[:, w0:w0 + nw, :], den[:, w0:w0 + nw, :]).then_inc(rcp_ready, 1)
                        dve.wait_ge(rcp_ready, 3 * T + (n - 2))
                        if i >= 2 and n == 0:
                            dve.wait_ge(tr_done, 2 * T - 2)
                        nc.vector.tensor_tensor(
                            ao[:, w0:w0 + nw, :].rearrange("p w (h m) -> p w h m", m=DIM), o[:, :, :, 0:DIM],
                            rcp[:, w0:w0 + nw, :].unsqueeze(3).to_broadcast([P, nw, HEADS_G, DIM]),
                            ALU.mult).then_inc(ao_ready, 1)
                if i % 2 == 0 and (i + 2) // 2 < ROWS:
                    r = (i + 2) // 2
                    row_low(grow(R0, i, r), r % 2)
                if i == TILES - 2 and not last_image:
                    group_norm_end(2 * b + 2, gn0)
                if i + 1 < TILES:
                    dve.wait_ge(raw_ready, T + 2)
                    if i >= 1:
                        dve.wait_ge(ktv_done, 2 * T - 1)
                    nc.vector.tensor_scalar(kr[:, par1, 0:C], raw[:, par1, 0:C], 0.0, None, ALU.max).then_inc(k_ready, 1)
                if 0 <= i < TILES:
                    for h in range(2):
                        dve.wait_ge(ktv_done, 2 * T + (h + 1))
                        if i >= 1:
                            for e in PLACE:
                                dve.wait_ge(placed[e], len(PLACE[e]) * T)
                        kv = ps[:, BANK_S[h], :]
                        nc.vector.tensor_tensor(
                            kvm[:, h, :, :, :].rearrange("p g s (i m) -> p (g s) i m", m=DIM + 1)[:, :, :, 0:DIM],
                            kv.rearrange("p (s i m) -> p s i m", i=HEADS_Q, m=DIM),
                            hm[:].unsqueeze(1).unsqueeze(3).to_broadcast([P, 2 * SLOTS, HEADS_Q, DIM]), ALU.mult)
                        nc.vector.tensor_tensor(
                            kvm[:, h, :, 0:NWIN, :].rearrange("p g s (i m) -> p g s i m", m=DIM + 1)[:, :, :, :, DIM],
                            kv.rearrange("p (g s) -> p g s", g=2)[:, :, NWIN * 32:NWIN * 32 + NWIN]
                            .unsqueeze(3).to_broadcast([P, 2, NWIN, HEADS_Q]),
                            hm[:].unsqueeze(1).unsqueeze(1).to_broadcast([P, 2, NWIN, HEADS_Q]),
                            ALU.mult).then_inc(masked, 1)
                    for h, q in PLACE["dve"]:
                        dve.wait_ge(masked, 2 * T + (h + 1))
                        if i >= 1:
                            dve.wait_ge(att_done, 3 * T)
                        s = slice(32 * q, 32 * q + 32)
                        nc.vector.tensor_copy(kvb[s, 2 * h:2 * h + 2, :, q * QW:(q + 1) * QW],
                                              kvm[s, h, :, 0:NWIN, :]).then_inc(placed["dve"], 1)
                if i % 2 == 0 and i < TILES:
                    r = i // 2
                    dve.wait_ge(qsum_ready, grow(R0, i, r) + 1)
                    if i >= 4:
                        dve.wait_ge(att_done, 3 * T - 6)
                    nc.vector.tensor_scalar(qs[:, MT:G, r % 2, 0:ROW_TOK],
                                            qsum.rearrange("p (m n) -> p m n", m=MT),
                                            POOL_SCALE, 0.0, ALU.mult, ALU.max).then_inc(qp_ready, 1)
                if not last_image:
                    if i == TILES - 2:
                        dve.wait_ge(qp_ready, (b + 1) * ROWS)
                        first_chunk(b + 1, (b + 1) % 2)
                    if i == TILES - 1:
                        product_inputs(b + 1, 0, 0, first=True)
                    if i == TILES:
                        low_parts((b + 1) * CONV_STEPS, 0)
                        dve.wait_ge(tr_done, 2 * T)
                        product_inputs(b + 1, 0, 1, first=True)

            nc.vector.memset(kvb[:], 0.0).then_inc(set_up, 1)
            nc.vector.memset(qs[:, :, :, ROW_TOK:], 0.0).then_inc(set_up, 1)
            dve.wait_ge(set_up, 2)
            dve.wait_ge(bn_loaded, DMA)
            nc.vector.tensor_scalar(bnt[:, 0, :], bnp[:, 3, :], BN_EPS, None, ALU.add).then_inc(bn_step, 1)
            dve.wait_ge(bn_step, 1)
            dve.wait_ge(bn_ready, 1)
            nc.vector.reciprocal(bnt[:, 2, :], bnt[:, 1, :]).then_inc(bn_step, 1)
            dve.wait_ge(bn_step, 2)
            nc.vector.tensor_tensor(bnt[:, 3, :], bnt[:, 2, :], bnt[:, 0, :], ALU.mult).then_inc(bn_step, 1)
            dve.wait_ge(bn_step, 3)
            nc.vector.tensor_tensor(bnt[:, 4, :], bnt[:, 3, :], bnt[:, 1, :], ALU.add).then_inc(bn_step, 1)
            dve.wait_ge(bn_step, 4)
            nc.vector.tensor_scalar(bnt[:, 5, :], bnt[:, 4, :], 0.5, None, ALU.mult).then_inc(bn_step, 1)
            dve.wait_ge(bn_step, 5)
            nc.vector.reciprocal(bnt[:, 2, :], bnt[:, 5, :]).then_inc(bn_step, 1)
            dve.wait_ge(bn_step, 6)
            nc.vector.tensor_tensor(bni[:], bnp[:, 0, :], bnt[:, 2, :], ALU.mult).then_inc(bn_step, 1)
            dve.wait_ge(bn_step, 7)
            nc.vector.tensor_tensor(bnt[:, 3, :], bnp[:, 2, :], bni[:], ALU.mult).then_inc(bn_step, 1)
            dve.wait_ge(bn_step, 8)
            nc.vector.tensor_tensor(bns[:], bnp[:, 1, :], bnt[:, 3, :], ALU.subtract).then_inc(bn_step, 1)
            for k in range(4):
                nc.vector.memset(dev[:, k, :], 0.0).then_inc(conv_added, 1)

            def w_do(n, ins):
                ins.then_inc(w_step, 1)
                dve.wait_ge(w_step, n)

            g0, gsum, g1, g2 = wprod
            dve.wait_ge(w_loaded, DMA)
            w_do(1, nc.vector.tensor_tensor(wouter, g0, g2, ALU.add))
            w_do(2, nc.vector.tensor_tensor(gsum, wouter, g1, ALU.add))
            w_do(3, nc.vector.tensor_scalar(gsum, gsum, 0.5, None, ALU.mult))
            w_do(4, nc.vector.tensor_tensor(g1, wouter, g1, ALU.subtract))
            w_do(5, nc.vector.tensor_scalar(g1, g1, 0.5, None, ALU.mult))

            def taps_low(k):
                dve.wait_ge(w_high, len(PRODUCTS))
                nc.vector.tensor_tensor(wc[:, 1, k], wprod[k], wc[:, 0, k].bitcast(F32),
                                        ALU.subtract).then_inc(w_ready, 1)

            taps_low(PRODUCTS[0])
            dve.wait_ge(x_loaded, KT * DMA)
            for c in range(CHUNKS):
                if c == CHUNKS - 1:
                    dve.wait_ge(x_tail_loaded, KT * DMA)
                stats_x(0, c).then_inc(st0_done, 1)
            dve.wait_ge(st0_done, CHUNKS)
            dve.wait_ge(conv_added, 4)
            group_norm_start(0, st0, gn0)
            group_norm_end(0, gn0)
            first_chunk(0, 0)
            product_inputs(0, 0, 0, first=True)
            product_inputs(0, 0, 1, first=True)
            low_parts(0, 0)
            for k in PRODUCTS[1:]:
                taps_low(k)
            dve.wait_ge(att_w_high, 2)
            nc.vector.tensor_tensor(wkv[:, 1], wkv_raw, wkv[:, 0].bitcast(F32), ALU.subtract).then_inc(att_w_low, 1)
            conv(0)
            group_norm_start(1, st1, gn1)
            group_norm_end(1, gn1)
            with dve.Fori(0, B - 1) as b:
                slots(dve, b, slot, False)
                conv(b + 1)
                group_norm_start(2 * b + 3, st1, gn1)
                group_norm_end(2 * b + 3, gn1)
            slots(dve, B - 1, slot, True)

        @block.gpsimd
        def _(pool):
            def slot(T, R0, i, b, c, last_image):
                if 0 <= i < TILES:
                    if i % 2 == 0:
                        pool.wait_ge(qsum_ready, alone(pool, grow(R0, i, i // 2) + 1))
                    elif i >= 5:
                        pool.wait_ge(out_ready, alone(pool, grow(R0, i, (i - 5) // 2) + 1))
                    for h, q in PLACE["pool"]:
                        pool.wait_ge(masked, alone(pool, 2 * T + (h + 1)))
                        if i >= 1:
                            pool.wait_ge(att_done, alone(pool, 3 * T))
                        s = slice(32 * q, 32 * q + 32)
                        nc.gpsimd.tensor_scalar(kvb[s, 2 * h:2 * h + 2, :, q * QW:(q + 1) * QW],
                                                kvm[s, h, :, 0:NWIN, :], 1.0, 0.0,
                                                ALU.mult, ALU.add).then_inc(placed["pool"], 1)
                if i % 2 == 1 and i + 1 < TILES:
                    r = (i + 1) // 2
                    n = grow(R0, i, r)
                    if i >= 1:
                        pool.wait_ge(placed["pool"], N_POOL * (T + 1))
                    pool.wait_ge(qraw_ready, n + 1)
                    col = qraw.rearrange("p (a c) -> p a c", c=WS)
                    hcol = qh.rearrange("p (a c) -> p a c", c=WS)
                    nc.gpsimd.tensor_tensor(qm, col[:, :, 1], col[:, :, 2], ALU.add).then_inc(q_step, 1)
                    pool.wait_ge(q_step, 6 * n + 1)
                    nc.gpsimd.tensor_tensor(hcol[:, :, 3], qm, col[:, :, 3], ALU.add)
                    nc.gpsimd.tensor_tensor(hcol[:, :, 0], qm, col[:, :, 0], ALU.add).then_inc(q_step, 1)
                    pool.wait_ge(q_step, 6 * n + 2)
                    nc.gpsimd.tensor_tensor(hcol[:, :, 1:3], hcol[:, :, 0:1].to_broadcast([P, MT * ROW_TOK // 4, 2]),
                                            col[:, :, 3:4].to_broadcast([P, MT * ROW_TOK // 4, 2]),
                                            ALU.add).then_inc(q_step, 1)
                    pool.wait_ge(q_step, 6 * n + 3)
                    row = qh.rearrange("p (a r c) -> p a r c", r=WS, c=WS)
                    srow = qsum.rearrange("p (a r c) -> p a r c", r=WS, c=WS)
                    mid = qm.rearrange("p (a c) -> p a c", c=WS)
                    nc.gpsimd.tensor_tensor(mid, row[:, :, 1, :], row[:, :, 2, :], ALU.add).then_inc(q_step, 1)
                    pool.wait_ge(q_step, 6 * n + 4)
                    if i >= 1:
                        pool.wait_ge(qp_ready, n)
                    nc.gpsimd.tensor_tensor(srow[:, :, 3, :], mid, row[:, :, 3, :], ALU.add).then_inc(q_step, 1)
                    nc.gpsimd.tensor_tensor(srow[:, :, 0, :], mid, row[:, :, 0, :], ALU.add).then_inc(q_step, 1)
                    pool.wait_ge(q_step, 6 * n + 6)
                    nc.gpsimd.tensor_tensor(srow[:, :, 1:3, :],
                                            srow[:, :, 0:1, :].to_broadcast([P, MT * WIN_PER_ROW, 2, WS]),
                                            row[:, :, 3:4, :].to_broadcast([P, MT * WIN_PER_ROW, 2, WS]),
                                            ALU.add).then_inc(qsum_ready, 1)
                if i % 2 == 0 and 0 <= (i - 4) // 2 < ROWS - 2:
                    r = (i - 4) // 2
                    pool.wait_ge(placed["pool"], N_POOL * (T + 1 if i < TILES else T))
                    add_row(b, grow(R0, i, r), lrow(c, i, r))

            def add_row(b, n, row):
                pool.wait_ge(y_ready, n + 1)
                for mt in range(MT):
                    xrow = xs_row(b % 2, mt, row).rearrange("p o (r w c) -> p (o w) r c", r=WS, c=WS)
                    last = nc.gpsimd.tensor_tensor(
                        xrow, yb[:, mt, :].rearrange("p (w r c) -> p w r c", r=WS, c=WS), xrow, ALU.add)
                last.then_inc(out_ready, 1)

            with pool.Fori(0, B) as b:
                slots(pool, b, slot, False)
                pool.wait_ge(placed["pool"], (b + 1) * (N_POOL * TILES))
                for row in (ROWS - 2, ROWS - 1):
                    add_row(b, b * ROWS + row, row)


def kernel(x, L0_conv_weight, L1_conv_qkv_w, L1_conv_proj_w, L1_conv_bn_gamma, L1_conv_bn_beta,
           L1_conv_bn_mean, L1_conv_bn_var):
    import concourse.bacc as bacc
    from concourse.bass_utils import run_bass_kernel_spmd

    def channels_first(w, split):
        return np.ascontiguousarray(w.reshape((split, P) + w.shape[1:]).swapaxes(0, 1))

    conv = channels_first(np.asarray(L0_conv_weight).reshape(C, C, TAPS * TAPS).transpose(1, 2, 0), KT)
    heads = np.asarray(L1_conv_qkv_w).reshape(C // DIM, 3, DIM, C).transpose(3, 1, 0, 2).reshape(C, 3 * C)
    qkv = channels_first(heads, KT)
    proj = channels_first(np.asarray(L1_conv_proj_w).T, G)
    bn = np.stack([np.asarray(v).reshape(MT, P).T for v in
                   (L1_conv_bn_gamma, L1_conv_bn_beta, L1_conv_bn_mean, L1_conv_bn_var)], axis=1)

    chan = np.arange(P)
    gavg = (chan[:, None] // GN_GROUP == chan[None, :] // GN_GROUP).astype(np.float32) / GN_GROUP
    tok = np.arange(TT)
    y, xx = tok % TOK // WS, tok % WS
    pool_m = ((tok[:, None] // TOK == tok[None, :] // TOK) & (abs(y[:, None] - y[None, :]) <= 2)
              & (abs(xx[:, None] - xx[None, :]) <= 2)).astype(np.float32)
    hmask = (chan[:, None] % 32 // DIM == np.arange(HEADS_Q)[None, :]).astype(np.float32)
    vinit = np.zeros((TT, SLOTS, 2 * C // 32, 32), np.float32)
    vinit[tok, NWIN, :, tok // TOK] = 1.0

    arrays = {
        "x": np.asarray(x).reshape(B, C, HW), "w_conv": conv,
        "w_q": np.ascontiguousarray(qkv[:, :, 0:C]), "w_kv": np.ascontiguousarray(qkv[:, :, C:]),
        "w_proj": proj, "bn": np.ascontiguousarray(bn), "gavg": gavg, "pool_m": pool_m,
        "ident": np.eye(P, dtype=np.float32), "hmask": hmask, "vinit": vinit.reshape(TT, SLOTS, 2, C),
    }
    nc = bacc.Bacc("TRN2", target_bir_lowering=False, num_devices=1)
    args = [nc.dram_tensor(n, a.shape, F32, kind="ExternalInput").ap() for n, a in arrays.items()]
    out = nc.dram_tensor("out", (B, C, H, W), F32, kind="ExternalOutput").ap()
    build(nc, *args, out.rearrange("b c h w -> b c (h w)"))
    r = run_bass_kernel_spmd(nc, [arrays], core_ids=[0])
    return r.results[0]["out"]
```
